# Optimizing a Trainium2 kernel written in Bass

```python
import numpy as np
import jax
import jax.numpy as jnp

def _softmax(x, axis=-1):
    return jax.nn.softmax(x, axis=axis)

def _gelu(x):
    return jax.nn.gelu(x, approximate=True)

def _silu(x):
    return jax.nn.silu(x)

def _sigmoid(x):
    return jax.nn.sigmoid(x)

def _layernorm(x, axis=-1, eps=1e-05):
    m = jnp.mean(x, axis=axis, keepdims=True)
    v = jnp.var(x, axis=axis, keepdims=True)
    return (x - m) / jnp.sqrt(v + eps)

def _scatter_add(tgt, idx, src, axis=0):
    return tgt.at[idx].add(src)

def _segment_sum(src, seg, n):
    return jax.ops.segment_sum(src, seg, n)
kernel_name = 'mk_audio_tower_d1_tok_audfeat512_r4_48f5ca'

def setup_inputs(seed: int=0):
    np.random.seed(seed)
    _w = jnp.asarray

    def _rec_inputs():
        import jax
        import jax.numpy as jnp
        _rk = jax.random.key(seed)
        x = -0.000520686 + 1.00062 * jax.random.normal(jax.random.fold_in(_rk, 1), (4, 32, 750), jnp.float32)
        return x
    x = _rec_inputs()

    def _L0_tok_setup():
        import jax, jax.numpy as jnp
        import numpy as np
        ALPHA = 0.1

        def ewma(y, alpha=ALPHA):
            y_t = jnp.swapaxes(y, 0, 1)

            def step(carry, xt):
                c = alpha * xt + (1.0 - alpha) * carry
                return (c, c)
            _, out = jax.lax.scan(step, y_t[0], y_t[1:])
            out = jnp.concatenate([y_t[:1], out], axis=0)
            return jnp.swapaxes(out, 0, 1)
        key = jax.random.key(seed)
        k1, k2, k3, k4, k5 = jax.random.split(key, 5)
        B, C, T, D = (32, 32, 512, 128)
        x = jax.random.normal(k1, (B, C, T), dtype=jnp.float32)
        W_ve = jax.random.normal(k2, (D, C), dtype=jnp.float32) * (1.0 / np.sqrt(C))
        b_ve = jax.random.normal(k3, (D,), dtype=jnp.float32) * 0.01
        W_lin = jax.random.normal(k4, (D, D), dtype=jnp.float32) * (1.0 / np.sqrt(D))
        b_lin = jax.random.normal(k5, (D,), dtype=jnp.float32) * 0.01
        return {'x': x, 'W_ve': W_ve, 'b_ve': b_ve, 'W_lin': W_lin, 'b_lin': b_lin}
    _L0_tok_all = _L0_tok_setup()
    _L0_tok_in = {k: v for k, v in _L0_tok_all.items() if k in ('W_ve', 'b_ve', 'W_lin', 'b_lin')}
    del _L0_tok_all

    def _L0_attn_setup():
        import jax, jax.numpy as jnp
        import numpy as np
        EPS = 1e-12

        def _l2norm(x):
            n = jnp.sqrt(jnp.sum(x * x, axis=-1, keepdims=True))
            return x / jnp.maximum(n, EPS)
        key = jax.random.key(seed)
        ks = jax.random.split(key, 8)
        B, T, V = (4, 512, 128)
        C, H, NB = (128, 4, 64)
        return {'x': jax.random.normal(ks[0], (B, T, V), dtype=jnp.float32), 'basis': jax.random.normal(ks[1], (V, 2 * NB), dtype=jnp.float32), 'shared_q_w': jax.random.normal(ks[2], (V, C), dtype=jnp.float32) * 0.02, 'shared_k_w': jax.random.normal(ks[3], (V, C), dtype=jnp.float32) * 0.02, 'v_coeffs': jax.random.normal(ks[4], (C, 2 * NB), dtype=jnp.float32) * 0.02, 'o_coeffs': jax.random.normal(ks[5], (C, 2 * NB), dtype=jnp.float32) * 0.02, 'decay_logits': jnp.linspace(1.0, 5.0, H, dtype=jnp.float32), 'out_scale': jnp.float32(0.1)}
    _L0_attn_all = _L0_attn_setup()
    _L0_attn_in = {k: v for k, v in _L0_attn_all.items() if k in ('basis', 'shared_q_w', 'shared_k_w', 'v_coeffs', 'o_coeffs', 'decay_logits', 'out_scale')}
    del _L0_attn_all

    def _L0_ffn_setup():
        import jax, jax.numpy as jnp
        import numpy as np
        T = 128
        B = 64
        C = 256

        def _triu_apply(x, W, b):
            Wm = jnp.tril(W)
            return jnp.einsum('bct,st->bcs', x, Wm) + b
        key = jax.random.key(seed)
        ks = jax.random.split(key, 5)
        x = jax.random.normal(ks[0], (B, C, T), dtype=jnp.float32)
        scale = 1.0 / jnp.sqrt(jnp.arange(1, T + 1, dtype=jnp.float32))[:, None]
        W1 = jax.random.uniform(ks[1], (T, T), jnp.float32, -1.0, 1.0) * scale
        b1 = jax.random.uniform(ks[2], (T,), jnp.float32, -1.0, 1.0) * scale[:, 0]
        W2 = jax.random.uniform(ks[3], (T, T), jnp.float32, -1.0, 1.0) * scale
        b2 = jax.random.uniform(ks[4], (T,), jnp.float32, -1.0, 1.0) * scale[:, 0]
        return {'x': x, 'W1': W1, 'b1': b1, 'W2': W2, 'b2': b2}
    _L0_ffn_all = _L0_ffn_setup()
    _L0_ffn_in = {k: v for k, v in _L0_ffn_all.items() if k in ('W1', 'b1', 'W2', 'b2')}
    del _L0_ffn_all
    return {'x': x, 'L0_tok_W_ve': _L0_tok_in['W_ve'], 'L0_tok_b_ve': _L0_tok_in['b_ve'], 'L0_tok_W_lin': _L0_tok_in['W_lin'], 'L0_tok_b_lin': _L0_tok_in['b_lin'], 'L0_attn_basis': _L0_attn_in['basis'], 'L0_attn_shared_q_w': _L0_attn_in['shared_q_w'], 'L0_attn_shared_k_w': _L0_attn_in['shared_k_w'], 'L0_attn_v_coeffs': _L0_attn_in['v_coeffs'], 'L0_attn_o_coeffs': _L0_attn_in['o_coeffs'], 'L0_attn_decay_logits': _L0_attn_in['decay_logits'], 'L0_attn_out_scale': _L0_attn_in['out_scale'], 'L0_ffn_W1': _L0_ffn_in['W1'], 'L0_ffn_b1': _L0_ffn_in['b1'], 'L0_ffn_W2': _L0_ffn_in['W2'], 'L0_ffn_b2': _L0_ffn_in['b2']}

def reference(x, L0_tok_W_ve, L0_tok_b_ve, L0_tok_W_lin, L0_tok_b_lin, L0_attn_basis, L0_attn_shared_q_w, L0_attn_shared_k_w, L0_attn_v_coeffs, L0_attn_o_coeffs, L0_attn_decay_logits, L0_attn_out_scale, L0_ffn_W1, L0_ffn_b1, L0_ffn_W2, L0_ffn_b2):
    import jax
    import jax.numpy as jnp

    def _L0_tok_ref(x, W_ve, b_ve, W_lin, b_lin):
        import jax, jax.numpy as jnp
        import numpy as np
        ALPHA = 0.1

        def ewma(y, alpha=ALPHA):
            y_t = jnp.swapaxes(y, 0, 1)

            def step(carry, xt):
                c = alpha * xt + (1.0 - alpha) * carry
                return (c, c)
            _, out = jax.lax.scan(step, y_t[0], y_t[1:])
            out = jnp.concatenate([y_t[:1], out], axis=0)
            return jnp.swapaxes(out, 0, 1)
        xt = jnp.transpose(x, (0, 2, 1))
        B, T, C = xt.shape
        x_diff = jnp.concatenate([jnp.zeros((B, 1, C), dtype=xt.dtype), xt[:, 1:, :] - xt[:, :-1, :]], axis=1)
        x_emb = jnp.einsum('btc,dc->btd', x_diff, W_ve) + b_ve
        x_lr = ewma(x_emb)
        x_rl = jnp.flip(ewma(jnp.flip(x_emb, axis=1)), axis=1)
        x_smooth = (x_lr + x_rl) * 0.5
        return jnp.einsum('btd,ed->bte', x_smooth, W_lin) + b_lin

    def _L0_attn_ref(x, basis, shared_q_w, shared_k_w, v_coeffs, o_coeffs, decay_logits, out_scale):
        import jax, jax.numpy as jnp
        import numpy as np
        EPS = 1e-12

        def _l2norm(x):
            n = jnp.sqrt(jnp.sum(x * x, axis=-1, keepdims=True))
            return x / jnp.maximum(n, EPS)
        B, T, V = x.shape
        H = decay_logits.shape[0]
        C = shared_q_w.shape[1]
        D = C // H
        v_w = basis @ v_coeffs.T
        o_w = basis @ o_coeffs.T
        q = _l2norm(x @ shared_q_w)
        k = _l2norm(x @ shared_k_w)
        v = x @ v_w
        q = q.reshape(B, T, H, D).transpose(0, 2, 1, 3)
        k = k.reshape(B, T, H, D).transpose(0, 2, 1, 3)
        v = v.reshape(B, T, H, D).transpose(0, 2, 1, 3)
        scores = jnp.einsum('bhqd,bhkd->bhqk', q, k)
        decay = jax.nn.sigmoid(decay_logits)
        pos = jnp.arange(T)
        diff = pos[None, :] - pos[:, None]
        mask = (diff > 0).astype(scores.dtype)
        expo = jnp.clip(diff.astype(jnp.float32) - 1.0, 0.0, None)
        decay_w = decay[:, None, None] ** expo[None] * mask[None]
        scores = scores * decay_w[None].astype(scores.dtype)
        retrieved = jnp.einsum('bhqk,bhkd->bhqd', scores, v)
        retrieved = retrieved.transpose(0, 2, 1, 3).reshape(B, T, C)
        return retrieved @ o_w.T * out_scale

    def _L0_ffn_ref(x, W1, b1, W2, b2):
        import jax, jax.numpy as jnp
        import numpy as np
        T = 128
        B = 64
        C = 256

        def _triu_apply(x, W, b):
            Wm = jnp.tril(W)
            return jnp.einsum('bct,st->bcs', x, Wm) + b
        h = _triu_apply(x, W1, b1)
        h = jax.nn.gelu(h, approximate=False)
        return _triu_apply(h, W2, b2)
    h = _L0_tok_ref(x, L0_tok_W_ve, L0_tok_b_ve, L0_tok_W_lin, L0_tok_b_lin)
    h = h + _L0_attn_ref(_layernorm(h, axis=-1), L0_attn_basis, L0_attn_shared_q_w, L0_attn_shared_k_w, L0_attn_v_coeffs, L0_attn_o_coeffs, L0_attn_decay_logits, L0_attn_out_scale)
    h = h + _L0_ffn_ref(_layernorm(h, axis=-1), L0_ffn_W1, L0_ffn_b1, L0_ffn_W2, L0_ffn_b2)
    return h

_drawn_inputs = setup_inputs


def setup_inputs(seed=0):
    import zlib

    import numpy as np

    out = dict(_drawn_inputs(seed))
    spreads = {}
    factors = {}
    for name, (base, spread) in spreads.items():
        noise = np.random.default_rng([zlib.crc32(name.encode()), seed]).standard_normal(out[name].shape)
        drawn = base * np.exp(spread * noise) if base else spread * noise
        out[name] = jnp.asarray(drawn.astype(out[name].dtype))
    for name, factor in factors.items():
        out[name] = (out[name] * factor).astype(out[name].dtype)
    return out
```

```python
from contextlib import ExitStack

import concourse.bass as bass
from concourse import mybir

F32 = mybir.dt.float32
F32R = mybir.dt.float32r
ALU = mybir.AluOpType
ACT = mybir.ActivationFunctionType

B, CH, T = 4, 32, 750
D = 128
H, HD = 4, 32
C = 125
NC = T // C
W4 = B * C
STK = 3 * CH + 2
ALPHA = 0.1
EPS_LN = 1e-5
EPS_L2 = 1e-12
LN_MAX = 2.0 ** 63
NBUF = 3
assert NC * C == T and B * CH == 128 and H * HD == D


def build(nc, x, W_ve, b_ve, W_lin, b_lin, basis, wq, wk, v_coeffs, o_coeffs, logits, out_scale,
          W1, b1, W2, b2, out):
    with ExitStack() as ctx:
        def sb(name, shape, dt=F32):
            return ctx.enter_context(nc.sbuf_tensor(name, shape, dt))

        def sem(name):
            return ctx.enter_context(nc.semaphore(name))

        IC = sb("ident_and_centring", [D, 2, D])
        ident, centre = IC[:, 0, :], IC[:, 1, :]
        block_mask = sb("block_mask", [D, H, HD])
        lo_rows = sb("lo_rows", [STK, 1])
        ones_blk = sb("ones_blk", [D, 2, B])
        w_lin = sb("w_lin", [D, D])
        VE = sb("ve_stack", [D, STK])
        BL = sb("b_lin_stack", [D, STK])
        wqk = sb("wqk", [D, 2 * D])
        w_basis = sb("w_basis", [D, D])
        w_vc = sb("w_vc", [D, D])
        w_oc = sb("w_oc", [D, D])
        w_1 = sb("w_1", [D, D])
        w_2 = sb("w_2", [D, D])
        b1_col = sb("b1_col", [D, 1])
        b2_row = sb("b2_row", [C, D])
        osc = sb("osc", [D, 1])
        b_lin_col = sb("b_lin_col", [D, 1])
        lin_T = sb("lin_T", [D, 2 * D])
        proj_T = sb("proj_T", [D, 3, STK])
        proj_rep = sb("proj_rep", [D, 3, B, CH])
        basis_ct = sb("basis_ct", [D, STK])
        tr4 = sb("tr4", [D, 4, D])
        w2_T = sb("w2_T", [D, D])
        o_T = sb("o_T", [D, D])
        w_hi = sb("w_hi", [STK, 4 * D], F32R)
        w_stk = sb("w_stk", [STK, 4 * D], F32R)
        Q0, K0, V0, H0 = 0, D, 2 * D, 3 * D
        gram = sb("gram", [D, 3, B, CH])
        gram_lin = sb("gram_lin", [D, 3])
        gram_c = sb("gram_c", [C, 3])

        lg_row = sb("lg_row", [C, H])
        lg_col = sb("lg_col", [D, 1])
        dec_row = sb("dec_row", [C, 4, H])
        dec_col = sb("dec_col", [D, 4])
        key_exp = sb("key_exp", [C, H])
        t_part = sb("t_part", [C, 1])
        t_left = sb("t_left", [D, C])
        t_diff = sb("t_diff", [C, C])
        t_full = sb("t_full", [D, 1])
        key_pow = sb("key_pow", [C, H])
        qry_pow = sb("qry_pow", [D, C])
        chunk_pow = sb("chunk_pow", [D, 1])
        dmask = sb("dmask", [C, H, C])

        xt = sb("xt", [D, T])
        xd = sb("xd", [D, T])
        keep = sb("keep", [D, T])
        half_last = sb("half_last", [D, 1])
        s_lr = sb("s_lr", [D, T])
        s_rl = sb("s_rl", [D, T])
        z = sb("z", [D, T])
        z_hi = sb("z_hi", [D, T], F32R)
        z_lo = sb("z_lo", [D, T], F32R)
        z_stk = sb("z_stk", [STK, NC, B, C], F32R)
        quad = sb("quad", [D, 3, T])
        ss = sb("ss", [C, 3, NC * B])
        rstd = sb("rstd", [C, NC * B])
        nrm = sb("nrm", [C, 3, NC * B])
        nrm2 = sb("nrm2", [C, 2, NC * B])
        rec = sb("rec", [C, 2, NC * B])
        sc_qk = sb("sc_qk", [C, 2, NC * B])
        sc_v = sb("sc_v", [C, NC * B])
        minus_half = sb("minus_half", [C, B])

        def bufs(name, shape):
            return [sb(f"{name}{n}", shape) for n in range(NBUF)]

        h_tok = bufs("h_tok", [C, B, D])
        k_dec = bufs("k_dec", [C, B, D])
        v_sc = bufs("v_sc", [C, B, D])
        qT = bufs("qT", [D, B, C])
        kT = bufs("kT", [D, B, C])
        q_dec = bufs("q_dec", [D, B, C])
        prob = [sb(f"prob{n}", [C, H, B, C]) for n in range(2)]
        rT = bufs("rT", [D, B, C])
        state = bufs("state", [D, B, D])
        state_m = bufs("state_m", [D, B, D])
        h2 = bufs("h2", [C, B, D])
        h2_b = bufs("h2_b", [C, B, D])
        bn6 = bufs("bn6", [C, B, 6])
        mv = bufs("mv", [C, B, 2])
        ve2 = bufs("ve2", [C, B])
        rstd2 = bufs("rstd2", [C, B])
        xn = bufs("xn", [C, B, D])
        xT = bufs("xT", [D, B, C])
        gT = bufs("gT", [D, B, C])
        y = bufs("y", [C, B, D])

        kv_ps = ctx.enter_context(nc.psum_tensor("kv_ps", [128, 1024], F32))
        hx_ps, qr_ps, kf_ps, f2_ps, s0_ps, s1_ps = (
            ctx.enter_context(nc.psum_tensor(n, [128, 512], F32))
            for n in ("hx_ps", "qr_ps", "kf_ps", "f2_ps", "s0_ps", "s1_ps"))
        st_ps, at_ps = kv_ps[:, 0:512], kv_ps[:, 512:1024]
        sc_ps = [s0_ps, s1_ps]

        x_in, lin_in, ve_in, bl_in, qk_in, bas_in, vo_in, f_in, row_in, dec_in = (
            sem(n) for n in ("x_in", "lin_in", "ve_in", "bl_in", "qk_in", "bas_in", "vo_in", "f_in",
                             "row_in", "dec_in"))
        pool_c, pool_pw, dv_c = sem("pool_c"), sem("pool_pw"), sem("dv_c")
        ident_ok, centre_ok, bl0_ok, lo_ok, mask_ok, tril_ok, ones_ok = (
            sem(n) for n in ("ident_ok", "centre_ok", "bl0_ok", "lo_ok", "mask_ok", "tril_ok", "ones_ok"))
        b1_in, osc_in, dec_u = sem("b1_in"), sem("osc_in"), sem("dec_u")
        ln_ok, diff_ok, dmask_e, std_ok = sem("ln_ok"), sem("diff_ok"), sem("dmask_e"), sem("std_ok")
        exp_ok, dec_ok, pow_ok, dmask_ok, keypow_ok, half_ok = (
            sem(n) for n in ("exp_ok", "dec_ok", "pow_ok", "dmask_ok", "keypow_ok", "half_ok"))
        ve_ok = sem("ve_ok")
        linT_ps, linT_ok, hrep_ps, projT_ps, projT_ok, qkrep_ps, qkT_ps, qkT_ok = (
            sem(n) for n in ("linT_ps", "linT_ok", "hrep_ps", "projT_ps", "projT_ok", "qkrep_ps",
                             "qkT_ps", "qkT_ok"))
        bct_ps, bct_ok, tr4_ps, tr4_ok, w2T_ps, w2T_ok, vo_ps, oT_ok = (
            sem(n) for n in ("bct_ps", "bct_ok", "tr4_ps", "tr4_ok", "w2T_ps", "w2T_ok", "vo_ps", "oT_ok"))
        rep_ok = sem("rep_ok")
        whi_ok, wstk_ok = sem("whi_ok"), sem("wstk_ok")
        gram_ps, gramc_ps, gram_ok, gramc_ok = (
            sem(n) for n in ("gram_ps", "gramc_ps", "gram_ok", "gramc_ok"))
        z_ok, zhi_ok, zlo_ok, zstk_v, zstk_d, zstk_a, zone_ok = (
            sem(n) for n in ("z_ok", "zhi_ok", "zlo_ok", "zstk_v", "zstk_d", "zstk_a", "zone_ok"))
        quad_ps, quad_ok, ss_ps, ss_ok, pw_ok, scale_ok, stat_v = (
            sem(n) for n in ("quad_ps", "quad_ok", "ss_ps", "ss_ok", "pw_ok", "scale_ok", "stat_v"))
        (qkT_s, qT_ok, kT_ok, kv_s, kd_ok, vs_ok, h_s, h_ok, score_s, prob_ok, qd_ok, rT_s, rT_ok, st_s, st_ok,
         stm_ok, at_s, h2_ok, bn_ok, mv_ok, ve2_ok, rstd2_ok, xn_ok, xT_s, xT_ok, f1_s, gT_ok, h2b_ok, f2_s,
         y_ok) = (
            sem(n) for n in ("qkT_s", "qT_ok", "kT_ok", "kv_s", "kd_ok", "vs_ok", "h_s", "h_ok", "score_s",
                             "prob_ok", "qd_ok", "rT_s", "rT_ok", "st_s", "st_ok", "stm_ok", "at_s", "h2_ok",
                             "bn_ok", "mv_ok", "ve2_ok", "rstd2_ok", "xn_ok", "xT_s", "xT_ok", "f1_s", "gT_ok",
                             "h2b_ok", "f2_s", "y_ok"))
        out_ok = [sem(f"out_ok{n}") for n in range(NBUF)]

        HALF = T // 2
        quads = [(a, half) for half in (1, 0) for a in range(3)]
        quad_bank = [qr_ps, kf_ps, s0_ps]
        block = ctx.enter_context(nc.Block())

        @block.sync
        def _(sp):
            sp.dma_start(xt[:, :], x.rearrange("b c t -> (b c) t")).then_inc(x_in, 16)
            sp.dma_start(VE[:, 0:CH], W_ve).then_inc(ve_in, 16)
            sp.dma_start(VE[:, 3 * CH:3 * CH + 1], b_ve.unsqueeze(1)).then_inc(ve_in, 16)
            sp.dma_start(wqk[:, 0:D], wq).then_inc(qk_in, 16)
            sp.dma_start(w_vc[:, :], v_coeffs).then_inc(vo_in, 16)
            sp.dma_start(w_1[:, :], W1).then_inc(f_in, 16)
            sp.dma_start(w_2[:, :], W2).then_inc(f_in, 16)
            sp.dma_start(b2_row[:, :], b2.unsqueeze(0).broadcast_to([C, D])).then_inc(row_in, 16)
            sp.wait_ge(zlo_ok, 1)
            for part, src in enumerate((z_hi, z_lo, z_hi)):
                for b in range(B):
                    sp.dma_start(z_stk[part * CH:(part + 1) * CH, 0:NC - 1, b, :].bitcast(F32),
                                 src[CH * b:CH * b + CH, 0:(NC - 1) * C].bitcast(F32).rearrange("p (c t) -> p c t", t=C))\
                        .then_inc(zstk_d, 16)
            for i in range(NC):
                c = NC - 1 - i
                sp.wait_ge(y_ok, i + 1)
                sp.dma_start(out[:, c * C:(c + 1) * C, :].rearrange("b t f -> t b f"),
                             y[i % NBUF][:, :, :]).then_inc(out_ok[i % NBUF], 16)
            for n in range(NBUF):
                sp.wait_ge(out_ok[n], 16 * (NC // NBUF))

        @block.gpsimd
        def _(pool):
            pool.memset(ident, 0.0).then_inc(pool_c, 1)
            pool.memset(BL[:, :], 0.0).then_inc(bl0_ok, 1)
            pool.wait_ge(pool_c, 1)
            pool.affine_select(out=ident, in_=ident, compare_op=ALU.not_equal, fill=1.0, base=0,
                               pattern=[[-1, D]], channel_multiplier=1).then_inc(ident_ok, 1)
            pool.wait_ge(ident_ok, 1)
            pool.tensor_scalar(centre, ident, -1.0 / D, None, ALU.add).then_inc(centre_ok, 1)
            pool.wait_ge(bl_in, 16)
            pool.wait_ge(bl0_ok, 1)
            pool.tensor_copy(BL[:, 3 * CH:STK], b_lin_col[:, 0:1].broadcast_to([D, 2])).then_inc(bl0_ok, 1)
            pool.memset(block_mask[:, :, :], 1.0).then_inc(pool_c, 1)
            pool.wait_ge(pool_c, 2)
            pool.affine_select(out=block_mask[:, :, :], in_=block_mask[:, :, :], compare_op=ALU.is_ge, fill=0.0,
                               base=0, pattern=[[-HD, H], [0, HD]], channel_multiplier=1).then_inc(pool_c, 1)
            pool.wait_ge(pool_c, 3)
            pool.affine_select(out=block_mask[:, :, :], in_=block_mask[:, :, :], compare_op=ALU.is_ge, fill=0.0,
                               base=HD - 1, pattern=[[HD, H], [0, HD]], channel_multiplier=-1)\
                .then_inc(mask_ok, 1)
            pool.wait_ge(mask_ok, 1)
            pool.tensor_copy(ones_blk[:, 1, :], block_mask[:, :, 0]).then_inc(ones_ok, 1)
            pool.tensor_scalar(ones_blk[:, 0, :], block_mask[:, :, 0], 1.0 / D, None, ALU.mult)\
                .then_inc(ones_ok, 1)
            pool.wait_ge(f_in, 32)
            for w in (w_1, w_2):
                pool.affine_select(out=w[:, :], in_=w[:, :], compare_op=ALU.is_ge, fill=0.0, base=0,
                                   pattern=[[-1, D]], channel_multiplier=1).then_inc(tril_ok, 1)
            pool.iota(t_diff[:, :], pattern=[[-1, C]], base=-1, channel_multiplier=1,
                      allow_small_or_imprecise_dtypes=True).then_inc(pool_pw, 1)
            pool.iota(t_part[:, :], pattern=[[0, 1]], base=0, channel_multiplier=1,
                      allow_small_or_imprecise_dtypes=True).then_inc(pool_pw, 1)
            pool.iota(t_left[:, :], pattern=[[-1, C]], base=C - 1, channel_multiplier=0,
                      allow_small_or_imprecise_dtypes=True).then_inc(pool_pw, 1)
            pool.memset(t_full[:, :], float(C)).then_inc(pool_pw, 1)
            pool.memset(minus_half[:, :], -0.5).then_inc(half_ok, 1)
            pool.wait_ge(pool_pw, 4)
            pool.tensor_scalar(t_diff[:, :], t_diff[:, :], 0.0, None, ALU.max).then_inc(diff_ok, 1)
            pool.wait_ge(dmask_e, 1)
            pool.affine_select(out=dmask[:, :, :], in_=dmask[:, :, :], compare_op=ALU.is_ge, fill=0.0, base=-1,
                               pattern=[[0, H], [-1, C]], channel_multiplier=1).then_inc(dmask_ok, 1)
            for i in range(NC):
                n = i % NBUF
                if i > 0:
                    pool.wait_ge(qT_ok, i + 1)
                    pool.wait_ge(pow_ok, 2)
                    if i > NBUF:
                        pool.wait_ge(rT_s, i - NBUF + 1)
                    pool.tensor_tensor(q_dec[n][:, :, :], qT[n][:, :, :],
                                       qry_pow[:, :].unsqueeze(1).broadcast_to([D, B, C]),
                                       ALU.mult).then_inc(qd_ok, 1)
                if i < NC - 1:
                    pool.wait_ge(st_ok, i + 1)
                    if i >= NBUF:
                        pool.wait_ge(rT_s, i - NBUF + 2)
                    pool.tensor_tensor(state_m[n][:, :, :], state[n][:, :, :],
                                       block_mask[:, :, :].rearrange("p h d -> p (h d)").unsqueeze(1)
                                       .broadcast_to([D, B, D]), ALU.mult).then_inc(stm_ok, 1)
                pool.wait_ge(mv_ok, B * (i + 1))
                pool.tensor_scalar(ve2[n][:, :], mv[n][:, :, 1], EPS_LN, None, ALU.add).then_inc(ve2_ok, 1)
                pool.wait_ge(ve2_ok, i + 1)
                pool.wait_ge(half_ok, 1)
                pool.tensor_tensor(rstd2[n][:, :], ve2[n][:, :], minus_half[:, :], ALU.pow)\
                    .then_inc(rstd2_ok, 1)
                pool.wait_ge(row_in, 16)
                if i >= NBUF:
                    pool.wait_ge(y_ok, i - NBUF + 1)
                pool.tensor_tensor(h2_b[n][:, :, :], h2[n][:, :, :],
                                   b2_row[:, :].unsqueeze(1).broadcast_to([C, B, D]), ALU.add)\
                    .then_inc(h2b_ok, 1)

        @block.scalar
        def _(act):
            act.dma_start(lg_row[:, :], logits.unsqueeze(0).broadcast_to([C, H])).then_inc(dec_in, 16)
            act.dma_start(lg_col[:, :], logits.unsqueeze(1).unsqueeze(2).broadcast_to([H, HD, 1]))\
                .then_inc(dec_in, 16)
            act.dma_start(w_lin[:, :], W_lin).then_inc(lin_in, 16)
            act.dma_start(b_lin_col[:, 0:1], b_lin.unsqueeze(1)).then_inc(bl_in, 16)
            act.dma_start(w_basis[:, :], basis).then_inc(bas_in, 16)
            act.dma_start(wqk[:, D:2 * D], wk).then_inc(qk_in, 16)
            act.dma_start(w_oc[:, :], o_coeffs).then_inc(vo_in, 16)
            act.dma_start(b1_col[:, :], b1.unsqueeze(1)).then_inc(b1_in, 16)
            act.dma_start(osc[:, :], out_scale.unsqueeze(0).broadcast_to([D, 1])).then_inc(osc_in, 16)
            act.wait_ge(dec_in, 32)
            act.activation(dec_row[:, 0, :], lg_row[:, :], ACT.Exp, scale=-1.0).then_inc(exp_ok, 1)
            act.activation(dec_col[:, 0:1], lg_col[:, :], ACT.Exp, scale=-1.0).then_inc(exp_ok, 1)
            act.wait_ge(dec_u, 2)
            act.activation(dec_row[:, 2, :], dec_row[:, 1, :], ACT.Ln).then_inc(ln_ok, 1)
            act.activation(dec_col[:, 2:3], dec_col[:, 1:2], ACT.Ln).then_inc(ln_ok, 1)
            act.wait_ge(linT_ps, 1)
            act.activation(lin_T[:, :], kv_ps[:, 0:2 * D], ACT.Copy).then_inc(linT_ok, 1)
            act.wait_ge(projT_ps, 1)
            act.activation(proj_T[:, 0, :], hx_ps[:, 0:STK], ACT.Copy).then_inc(projT_ok, 1)
            act.wait_ge(dec_ok, 3)
            act.wait_ge(diff_ok, 1)
            for h in range(H):
                ins = act.activation(dmask[:, h, :], t_diff[:, :], ACT.Exp, scale=dec_row[:, 3, h:h + 1])
            ins.then_inc(dmask_e, 1)
            act.activation(key_pow[:, :], key_exp[:, :], ACT.Exp).then_inc(keypow_ok, 1)
            act.activation(qry_pow[:, :], t_left[:, :], ACT.Exp, scale=dec_col[:, 3:4]).then_inc(pow_ok, 1)
            act.activation(chunk_pow[:, :], t_full[:, :], ACT.Exp, scale=dec_col[:, 3:4]).then_inc(pow_ok, 1)
            act.wait_ge(bct_ps, 1)
            act.activation(basis_ct[:, :], f2_ps[:, 0:STK], ACT.Copy).then_inc(bct_ok, 1)
            act.wait_ge(tr4_ps, 1)
            act.activation(tr4[:, :, :].rearrange("p a b -> p (a b)"), s0_ps[:, :], ACT.Copy)\
                .then_inc(tr4_ok, 1)

            act.wait_ge(zhi_ok, 1)
            for b in range(B):
                act.activation(z_stk[2 * CH:3 * CH, NC - 1, b, :],
                               z_hi[CH * b:CH * b + CH, (NC - 1) * C:T].bitcast(F32), ACT.Copy)\
                    .then_inc(zstk_a, 1)
            act.wait_ge(vo_ps, 2)
            act.wait_ge(osc_in, 16)
            act.activation(o_T[:, :], kv_ps[:, D:2 * D], ACT.Copy, scale=osc[:, 0:1]).then_inc(oT_ok, 1)
            act.wait_ge(w2T_ps, 1)
            act.activation(w2_T[:, :], at_ps[:, 0:D], ACT.Copy).then_inc(w2T_ok, 1)
            act.wait_ge(ss_ok, 3)
            act.activation(nrm[:, :, :], ss[:, :, :], ACT.Sqrt).then_inc(pw_ok, 1)

            def ffn_in(i):
                act.wait_ge(xT_s, i + 1)
                if i >= NBUF:
                    act.wait_ge(f1_s, i - NBUF + 1)
                act.activation(xT[i % NBUF][:, :, :].rearrange("p b t -> p (b t)"), hx_ps[:, 0:W4], ACT.Copy)\
                    .then_inc(xT_ok, 1)

            def ffn_gelu(i):
                act.wait_ge(f1_s, i + 1)
                if i == 0:
                    act.wait_ge(b1_in, 16)
                if i >= NBUF:
                    act.wait_ge(f2_s, i - NBUF + 1)
                act.activation(gT[i % NBUF][:, :, :].rearrange("p b t -> p (b t)"), kf_ps[:, 0:W4], ACT.Gelu,
                               bias=b1_col[:, 0:1]).then_inc(gT_ok, 1)

            for i in range(NC):
                n = i % NBUF
                act.wait_ge(qkT_s, 2 * i + 1)
                if i >= NBUF:
                    act.wait_ge(qd_ok, i - NBUF)
                    act.wait_ge(score_s, H * (i - NBUF + 1))
                act.activation(qT[n][:, :, :].rearrange("p b t -> p (b t)"), qr_ps[:, 0:W4], ACT.Copy)\
                    .then_inc(qT_ok, 1)
                act.wait_ge(qkT_s, 2 * i + 2)
                act.activation(kT[n][:, :, :].rearrange("p b t -> p (b t)"), kf_ps[:, 0:W4], ACT.Copy)\
                    .then_inc(kT_ok, 1)
                act.wait_ge(h_s, i + 1)
                if i >= NBUF:
                    act.wait_ge(h2_ok, B * (i - NBUF + 1))
                act.activation(h_tok[n][:, :, :].rearrange("p b f -> p (b f)"), hx_ps[0:C, :], ACT.Copy)\
                    .then_inc(h_ok, 1)
                if i > 0:
                    ffn_in(i - 1)
                act.wait_ge(rT_s, i + 1)
                if i >= NBUF:
                    act.wait_ge(at_s, i - NBUF + 1)
                act.activation(rT[n][:, :, :].rearrange("p b t -> p (b t)"), qr_ps[:, 0:W4], ACT.Copy)\
                    .then_inc(rT_ok, 1)
                if i > 0:
                    ffn_gelu(i - 1)
            ffn_in(NC - 1)
            ffn_gelu(NC - 1)

        @block.vector
        def _(dve):
            dve.memset(keep[:, :], 1.0 - ALPHA).then_inc(dv_c, 1)
            dve.memset(xd[:, 0:1], 0.0).then_inc(dv_c, 1)
            dve.memset(lo_rows[:, :], 0.0).then_inc(lo_ok, 1)
            dve.memset(z_stk[3 * CH:STK, :, :, :].bitcast(F32), 1.0).then_inc(zone_ok, 1)
            dve.wait_ge(lo_ok, 1)
            dve.memset(lo_rows[2 * CH:3 * CH, :], -1.0).then_inc(lo_ok, 1)
            dve.wait_ge(ident_ok, 1)
            dve.tensor_scalar(lo_rows[3 * CH:STK, :], ident[3 * CH:STK, STK - 1:STK], -1.0, None, ALU.mult)\
                .then_inc(lo_ok, 1)
            dve.wait_ge(ve_in, 32)
            dve.tensor_copy(VE[:, CH:3 * CH].rearrange("p (a c) -> p a c", a=2),
                            VE[:, 0:CH].unsqueeze(1).broadcast_to([D, 2, CH])).then_inc(ve_ok, 1)
            dve.tensor_copy(VE[:, 3 * CH + 1:STK], VE[:, 3 * CH:3 * CH + 1]).then_inc(ve_ok, 1)
            dve.wait_ge(exp_ok, 2)
            dve.tensor_scalar(dec_row[:, 1, :], dec_row[:, 0, :], 1.0, LN_MAX, ALU.add, ALU.min).then_inc(dec_u, 1)
            dve.tensor_scalar(dec_col[:, 1:2], dec_col[:, 0:1], 1.0, LN_MAX, ALU.add, ALU.min).then_inc(dec_u, 1)
            dve.wait_ge(x_in, 16)
            dve.tensor_tensor(xd[:, 1:T], xt[:, 1:T], xt[:, 0:T - 1], ALU.subtract).then_inc(dv_c, 1)
            dve.wait_ge(dv_c, 3)
            dve.tensor_scalar(half_last[:, :], xd[:, T - 1:T], 0.5, None, ALU.mult).then_inc(dv_c, 1)
            dve.tensor_scalar(xt[:, :], xd[:, :], 0.5 * ALPHA, None, ALU.mult).then_inc(dv_c, 1)
            dve.wait_ge(dv_c, 5)
            dve.tensor_tensor_scan(s_lr[:, :], keep[:, :], xt[:, :], 0.0, ALU.mult, ALU.add).then_inc(dv_c, 1)
            dve.tensor_tensor_scan(s_rl[:, ::-1], keep[:, :], xt[:, ::-1], half_last[:, 0:1], ALU.mult,
                                   ALU.add).then_inc(dv_c, 1)
            dve.wait_ge(dv_c, 7)
            dve.tensor_tensor(z[:, :], s_lr[:, :], s_rl[:, :], ALU.add).then_inc(z_ok, 1)
            dve.wait_ge(z_ok, 1)
            dve.tensor_copy(z_hi[:, :], z[:, :]).then_inc(zhi_ok, 1)
            dve.wait_ge(zhi_ok, 1)
            dve.tensor_tensor(z_lo[:, :], z[:, :], z_hi[:, :].bitcast(F32), ALU.subtract).then_inc(zlo_ok, 1)

            dve.wait_ge(ln_ok, 2)
            dve.tensor_scalar(dec_row[:, 3, :], dec_row[:, 2, :], -1.0, None, ALU.mult).then_inc(dec_ok, 1)
            dve.tensor_scalar(dec_col[:, 3:4], dec_col[:, 2:3], -1.0, None, ALU.mult).then_inc(dec_ok, 1)
            dve.wait_ge(pool_pw, 4)
            dve.tensor_scalar(key_exp[:, :], dec_row[:, 2, :], t_part[:, 0:1], -1.0, ALU.mult, ALU.mult)\
                .then_inc(dec_ok, 1)
            for part, src in ((0, z_hi), (1, z_lo)):
                dve.wait_ge(zlo_ok, 1)
                for b in range(B):
                    dve.tensor_copy(z_stk[part * CH:(part + 1) * CH, NC - 1, b, :],
                                    src[CH * b:CH * b + CH, (NC - 1) * C:T].bitcast(F32)).then_inc(zstk_v, 1)

            def stack_w(ps, c0, c1, k):
                dve.tensor_copy(w_hi[:, c0:c1], ps).then_inc(whi_ok, 1)
                dve.wait_ge(whi_ok, k)
                if k == 1:
                    dve.wait_ge(lo_ok, 3)
                dve.scalar_tensor_tensor(out=w_stk[:, c0:c1], in0=w_hi[:, c0:c1].bitcast(F32),
                                         scalar=lo_rows[:, 0:1], in1=ps, op0=ALU.mult, op1=ALU.add)\
                    .then_inc(wstk_ok, 1)
            dve.wait_ge(qkrep_ps, 1)
            stack_w(qr_ps[0:STK, 0:2 * D], Q0, V0, 1)
            dve.wait_ge(vo_ps, 1)
            stack_w(f2_ps[0:STK, 128:256], V0, H0, 2)
            dve.wait_ge(hrep_ps, 1)
            stack_w(s1_ps[0:STK, 256:384], H0, H0 + D, 3)
            dve.wait_ge(qkT_ps, 1)
            dve.tensor_copy(proj_T[:, 1:3, :].rearrange("p a b -> p (a b)"), kf_ps[:, 0:2 * STK])\
                .then_inc(qkT_ok, 1)
            dve.wait_ge(qkT_ok, 1)
            dve.wait_ge(projT_ok, 1)
            dve.tensor_copy(proj_rep[:, :, :, :], proj_T[:, :, 0:CH].unsqueeze(2).broadcast_to([D, 3, B, CH]))\
                .then_inc(rep_ok, 1)
            dve.wait_ge(gram_ps, 1)
            dve.wait_ge(mask_ok, 1)
            g3 = hx_ps[:, 0:3 * STK].rearrange("p (a b) -> p a b", a=3)
            for a in range(3):
                dve.tensor_tensor(gram[:, a, :, :], g3[:, a, 0:CH].unsqueeze(1).broadcast_to([D, B, CH]),
                                  block_mask[:, :, :], ALU.mult).then_inc(gram_ok, 1)
            dve.tensor_scalar(gram_lin[:, :], g3[:, :, 3 * CH], 2.0, None, ALU.mult).then_inc(gram_ok, 1)
            dve.wait_ge(gramc_ps, 1)
            dve.tensor_scalar(gram_c[:, 0:1], s1_ps[0:C, 128:129], 1.0 / D, EPS_LN, ALU.mult, ALU.add)\
                .then_inc(gramc_ok, 1)
            dve.tensor_copy(gram_c[:, 1:3], s1_ps[0:C, 129:131]).then_inc(gramc_ok, 1)
            dve.wait_ge(gram_ok, 4)
            for k, (a, half) in enumerate(quads):
                dve.wait_ge(quad_ps, k + 1)
                dve.scalar_tensor_tensor(out=quad[:, a, half * HALF:(half + 1) * HALF],
                                         in0=quad_bank[k % 3][:, 0:HALF], scalar=gram_lin[:, a:a + 1],
                                         in1=z[:, half * HALF:(half + 1) * HALF], op0=ALU.add, op1=ALU.mult)\
                    .then_inc(quad_ok, 1)
            dve.wait_ge(ss_ps, 1)
            dve.wait_ge(gramc_ok, 2)
            for a in range(3):
                dve.tensor_scalar(ss[:, a, :], f2_ps[0:C, 24 * a:24 * a + 24], gram_c[:, a:a + 1],
                                  EPS_LN if a == 0 else 0.0, ALU.add, ALU.max).then_inc(ss_ok, 1)
            dve.wait_ge(pw_ok, 1)
            dve.reciprocal(rstd[:, :], nrm[:, 0, :]).then_inc(std_ok, 1)
            dve.wait_ge(std_ok, 1)
            rb = rstd[:, :].unsqueeze(1).broadcast_to([C, 2, NC * B])
            dve.tensor_tensor(nrm2[:, :, :], nrm[:, 1:3, :], rb, ALU.mult).then_inc(stat_v, 1)
            dve.wait_ge(stat_v, 1)
            dve.tensor_scalar(nrm[:, 1:3, :], nrm2[:, :, :], EPS_L2, None, ALU.max).then_inc(stat_v, 1)
            dve.wait_ge(stat_v, 2)
            dve.reciprocal(rec[:, :, :], nrm[:, 1:3, :]).then_inc(stat_v, 1)
            dve.wait_ge(stat_v, 3)
            dve.tensor_tensor(sc_qk[:, :, :], rec[:, :, :], rb, ALU.mult).then_inc(stat_v, 1)
            dve.wait_ge(stat_v, 4)
            dve.tensor_tensor(sc_v[:, :], sc_qk[:, 1, :], rstd[:, :], ALU.mult).then_inc(scale_ok, 1)

            def last_sum(i):
                n = i % NBUF
                dve.wait_ge(f2_s, i + 1)
                dve.wait_ge(h2b_ok, i + 1)
                if i >= NBUF:
                    dve.wait_ge(out_ok[n], 16 * (i // NBUF))
                dve.tensor_tensor(y[n][:, :, :], f2_ps[0:C, :].rearrange("p (b f) -> p b f", b=B),
                                  h2_b[n][:, :, :], ALU.add).then_inc(y_ok, 1)

            for i in range(NC):
                n, c = i % NBUF, NC - 1 - i
                kv = kv_ps[0:C, :].rearrange("p (b f) -> p b f", b=B)
                tok = slice(c * B, c * B + B)
                if i < NC - 1:
                    dve.wait_ge(kv_s, 2 * i + 2)
                    if i == 0:
                        dve.wait_ge(keypow_ok, 1)
                    if i >= NBUF:
                        dve.wait_ge(st_s, i - NBUF + 1)
                    dve.tensor_tensor(k_dec[n][:, :, :].rearrange("p b (h d) -> p b h d", h=H),
                                      kv[:, :, 0:D].rearrange("p b (h d) -> p b h d", h=H),
                                      key_pow[:, :].unsqueeze(1).unsqueeze(3).broadcast_to([C, B, H, HD]),
                                      ALU.mult).then_inc(kd_ok, 1)
                dve.wait_ge(kv_s, 2 * i + 2)
                if i == 0:
                    dve.wait_ge(scale_ok, 1)
                if i >= NBUF:
                    dve.wait_ge(rT_s, i - NBUF + 1)
                dve.tensor_tensor(v_sc[n][:, :, :], kv[:, :, D:2 * D],
                                  sc_v[:, tok].unsqueeze(2).broadcast_to([C, B, D]), ALU.mult)\
                    .then_inc(vs_ok, 1)
                if i == 0:
                    dve.wait_ge(dmask_ok, 1)
                if i >= 2:
                    dve.wait_ge(rT_s, i - 1)
                for h in range(H):
                    dve.wait_ge(score_s, H * i + h + 1)
                    dve.tensor_tensor(prob[i % 2][:, h, :, :],
                                      sc_ps[h % 2][0:C, 0:W4].rearrange("p (b t) -> p b t", b=B),
                                      dmask[:, h, :].unsqueeze(1).broadcast_to([C, B, C]), ALU.mult)\
                        .then_inc(prob_ok, 1)
                if i < NC - 1:
                    dve.wait_ge(st_s, i + 1)
                    new = state[n][:, :, :].rearrange("p b f -> p (b f)")
                    if i >= NBUF:
                        dve.wait_ge(stm_ok, i - NBUF + 1)
                    if i == 0:
                        dve.tensor_copy(new, st_ps).then_inc(st_ok, 1)
                    else:
                        dve.wait_ge(st_ok, i)
                        dve.wait_ge(pow_ok, 2)
                        dve.scalar_tensor_tensor(
                            out=new, in0=state[(i - 1) % NBUF][:, :, :].rearrange("p b f -> p (b f)"),
                            scalar=chunk_pow[:, 0:1], in1=st_ps, op0=ALU.mult, op1=ALU.add).then_inc(st_ok, 1)
                if i > 0:
                    last_sum(i - 1)
                dve.wait_ge(at_s, i + 1)
                dve.wait_ge(h_ok, i + 1)
                if i >= NBUF:
                    dve.wait_ge(h2b_ok, i - NBUF + 1)
                for b in range(B):
                    dve.scalar_tensor_tensor(out=h2[n][:, b, :], in0=at_ps[0:C, b * D:(b + 1) * D],
                                             scalar=sc_qk[:, 0, c * B + b:c * B + b + 1],
                                             in1=h_tok[n][:, b, :], op0=ALU.mult, op1=ALU.add)\
                        .then_inc(h2_ok, 1)
                for b in range(B):
                    dve.wait_ge(h2_ok, B * i + b + 1)
                    ins = dve.bn_stats(bn6[n][:, b, :], h2[n][:, b, :])
                    ins.then_inc(bn_ok, 1)
                for b in range(B):
                    dve.wait_ge(bn_ok, B * i + b + 1)
                    dve.bn_aggr(mv[n][:, b, :], bn6[n][:, b, :]).then_inc(mv_ok, 1)
                dve.wait_ge(rstd2_ok, i + 1)
                if i >= NBUF:
                    dve.wait_ge(xT_s, i - NBUF + 1)
                for b in range(B):
                    ins = dve.tensor_scalar(xn[n][:, b, :], h2[n][:, b, :], mv[n][:, b, 0:1],
                                            rstd2[n][:, b:b + 1], ALU.subtract, ALU.mult)
                    ins.then_inc(xn_ok, 1)
            last_sum(NC - 1)

        @block.tensor
        def _(pe):
            pe.wait_ge(lin_in, 16)
            pe.wait_ge(centre_ok, 1)
            pe.matmul(kv_ps[:, 0:2 * D], w_lin[:, :], IC[:, :, :].rearrange("p a b -> p (a b)"),
                      start=True, stop=True).then_inc(linT_ps, 1)
            pe.wait_ge(linT_ok, 1)
            pe.wait_ge(ve_ok, 2)
            pe.wait_ge(bl0_ok, 2)
            pe.matmul(hx_ps[:, 0:STK], lin_T[:, D:2 * D], VE[:, :], start=True, stop=False)
            pe.matmul(hx_ps[:, 0:STK], centre, BL[:, :], start=False, stop=True).then_inc(projT_ps, 1)
            pe.matmul(s1_ps[0:STK, 256:384], VE[:, :], lin_T[:, 0:D], start=True, stop=False)
            pe.matmul(s1_ps[0:STK, 256:384], BL[:, :], ident, start=False, stop=True).then_inc(hrep_ps, 1)
            pe.wait_ge(projT_ok, 1)
            pe.wait_ge(qk_in, 32)
            pe.matmul(qr_ps[0:STK, 0:2 * D], proj_T[:, 0, :], wqk[:, :], start=True, stop=True)\
                .then_inc(qkrep_ps, 1)
            pe.wait_ge(bas_in, 16)
            pe.matmul(f2_ps[:, 0:STK], w_basis[:, :], proj_T[:, 0, :], start=True, stop=True)\
                .then_inc(bct_ps, 1)
            pe.matmul(kf_ps[:, 0:STK], wqk[:, 0:D], proj_T[:, 0, :], start=True, stop=True)
            pe.matmul(kf_ps[:, STK:2 * STK], wqk[:, D:2 * D], proj_T[:, 0, :], start=True, stop=True)\
                .then_inc(qkT_ps, 1)
            pe.wait_ge(vo_in, 32)
            pe.wait_ge(tril_ok, 2)
            for j, w in enumerate((w_vc, w_oc, w_basis, w_1)):
                ins = pe.transpose(s0_ps[:, j * D:(j + 1) * D], w[:, :], ident)
            ins.then_inc(tr4_ps, 1)
            pe.wait_ge(tr4_ok, 1)
            pe.wait_ge(bct_ok, 1)
            pe.matmul(f2_ps[0:STK, 128:256], basis_ct[:, :], tr4[:, 0, :], start=True, stop=True)\
                .then_inc(vo_ps, 1)
            pe.matmul(kv_ps[:, D:2 * D], tr4[:, 1, :], tr4[:, 2, :], start=True, stop=True).then_inc(vo_ps, 1)
            pe.wait_ge(rep_ok, 1)
            for a in range(3):
                ins = pe.matmul(hx_ps[:, a * STK:(a + 1) * STK],
                                proj_rep[:, a, :, :].rearrange("p b c -> p (b c)"),
                                proj_T[:, a, :], start=True, stop=True)
            ins.then_inc(gram_ps, 1)
            pe.wait_ge(wstk_ok, 3)
            for a in range(3):
                ins = pe.matmul(s1_ps[0:C, 128 + a:129 + a],
                                proj_T[:, a, 3 * CH:3 * CH + 1].broadcast_to([D, C]),
                                proj_T[:, a, 3 * CH:3 * CH + 1], start=True, stop=True)
            ins.then_inc(gramc_ps, 1)
            pe.transpose(at_ps[:, 0:D], w_2[:, :], ident).then_inc(w2T_ps, 1)

            def project_qk(i):
                c = NC - 1 - i
                zc = z_stk[:, c, :, :].rearrange("p b t -> p (b t)")
                if i > 0:
                    pe.wait_ge(rT_ok, i)
                pe.matmul(qr_ps[:, 0:W4], w_stk[:, Q0:Q0 + D], zc, start=True, stop=True).then_inc(qkT_s, 1)
                if i > 1:
                    pe.wait_ge(gT_ok, i - 1)
                pe.matmul(kf_ps[:, 0:W4], w_stk[:, K0:K0 + D], zc, start=True, stop=True).then_inc(qkT_s, 1)

            def project_tokens(i):
                c = NC - 1 - i
                for b in range(B):
                    if i > 0 and b == 0:
                        pe.wait_ge(st_ok, i)
                    if i > 0 and b == 2:
                        pe.wait_ge(h2_ok, B * i)
                    ins = pe.matmul(kv_ps[0:C, b * 2 * D:(b + 1) * 2 * D], z_stk[:, c, b, :],
                                    w_stk[:, K0:K0 + 2 * D], start=True, stop=True)
                    if b % 2:
                        ins.then_inc(kv_s, 1)
                if i > 1:
                    pe.wait_ge(xT_ok, i - 1)
                for b in range(B):
                    ins = pe.matmul(hx_ps[0:C, b * D:(b + 1) * D], z_stk[:, c, b, :],
                                    w_stk[:, H0:H0 + D], start=True, stop=True)
                ins.then_inc(h_s, 1)

            def score(i, h):
                n = i % NBUF
                if h == 0:
                    pe.wait_ge(qT_ok, i + 1)
                    pe.wait_ge(kT_ok, i + 1)
                if H * i + h >= 2:
                    pe.wait_ge(prob_ok, H * i + h - 1)
                rows = slice(h * HD, (h + 1) * HD)
                for b in range(B):
                    ins = pe.matmul(sc_ps[h % 2][0:C, b * C:(b + 1) * C], kT[n][rows, b, :], qT[n][rows, b, :],
                                    start=True, stop=True)
                ins.then_inc(score_s, 1)

            def retrieve(i):
                n = i % NBUF
                if i > 0:
                    pe.wait_ge(qd_ok, i)
                    pe.wait_ge(stm_ok, i)
                    for b in range(B):
                        pe.matmul(qr_ps[:, b * C:(b + 1) * C], state_m[(i - 1) % NBUF][:, b, :],
                                  q_dec[n][:, b, :], start=(b == 0), stop=False, skip_group_check=True)
                pe.wait_ge(vs_ok, i + 1)
                for b in range(B):
                    if b == 0:
                        pe.wait_ge(prob_ok, H * (i + 1))
                    for h in range(H):
                        cols = slice(h * HD, (h + 1) * HD)
                        ins = pe.matmul(qr_ps[cols, b * C:(b + 1) * C], v_sc[n][:, b, cols],
                                        prob[i % 2][:, h, b, :], start=(i == 0 and b == 0),
                                        stop=(b == B - 1), skip_group_check=True)
                ins.then_inc(rT_s, 1)

            def carry(i):
                n = i % NBUF
                pe.wait_ge(kd_ok, i + 1)
                pe.wait_ge(vs_ok, i + 1)
                for b in range(B):
                    ins = pe.matmul(st_ps[:, b * D:(b + 1) * D], k_dec[n][:, b, :], v_sc[n][:, b, :],
                                    start=True, stop=True)
                ins.then_inc(st_s, 1)

            def attention_out(i):
                n = i % NBUF
                pe.wait_ge(rT_ok, i + 1)
                if i == NC - 1:
                    pe.wait_ge(vs_ok, i + 1)
                if i == 0:
                    pe.wait_ge(oT_ok, 1)
                for b in range(B):
                    ins = pe.matmul(at_ps[0:C, b * D:(b + 1) * D], rT[n][:, b, :], o_T[:, :],
                                    start=True, stop=True)
                ins.then_inc(at_s, 1)

            def ffn_turn(i):
                n = i % NBUF
                pe.wait_ge(h_ok, min(i + 2, NC))
                for b in range(B):
                    pe.wait_ge(xn_ok, B * i + b + 1)
                    ins = pe.transpose(hx_ps[:, b * C:(b + 1) * C], xn[n][:, b, :], ident[0:C, 0:C])
                ins.then_inc(xT_s, 1)

            def ffn_1(i):
                pe.wait_ge(xT_ok, i + 1)
                pe.wait_ge(kT_ok, min(i + 2, NC))
                pe.matmul(kf_ps[:, 0:W4], tr4[:, 3, :], xT[i % NBUF][:, :, :].rearrange("p b t -> p (b t)"),
                          start=True, stop=True).then_inc(f1_s, 1)

            def ffn_2(i):
                n = i % NBUF
                pe.wait_ge(gT_ok, i + 1)
                if i == 0:
                    pe.wait_ge(w2T_ok, 1)
                if i > 0:
                    pe.wait_ge(y_ok, i)
                for b in range(B):
                    ins = pe.matmul(f2_ps[0:C, b * D:(b + 1) * D], gT[n][:, b, :], w2_T[:, :],
                                    start=True, stop=True)
                ins.then_inc(f2_s, 1)

            def token_stats():
                pe.wait_ge(gram_ok, 4)
                pe.wait_ge(z_ok, 1)
                for k, (a, half) in enumerate(quads):
                    if k >= 3:
                        pe.wait_ge(quad_ok, k - 2)
                    pe.matmul(quad_bank[k % 3][:, 0:HALF],
                              gram[:, a, :, :].rearrange("p b c -> p (b c)"),
                              z[:, half * HALF:(half + 1) * HALF], start=True, stop=True).then_inc(quad_ps, 1)
                pe.wait_ge(ones_ok, 2)
                for half in (1, 0):
                    pe.wait_ge(quad_ok, 3 if half else 6)
                    for a in range(3):
                        for c in range(half * NC // 2, (half + 1) * NC // 2):
                            ins = pe.matmul(f2_ps[0:C, (a * NC + c) * B:(a * NC + c + 1) * B],
                                            quad[:, a, c * C:(c + 1) * C], ones_blk[:, min(a, 1), :],
                                            start=True, stop=True)
                ins.then_inc(ss_ps, 1)

            token_stats()
            pe.wait_ge(zone_ok, 1)
            pe.wait_ge(zstk_v, 2 * B)
            pe.wait_ge(zstk_a, B)
            pe.wait_ge(w2T_ok, 1)
            for i in range(NC):
                if i == 1:
                    pe.wait_ge(zstk_d, 16 * 3 * B)
                project_qk(i)
                project_tokens(i)
                for h in range(H):
                    score(i, h)
                if i > 0:
                    ffn_turn(i - 1)
                    ffn_1(i - 1)
                retrieve(i)
                if i < NC - 1:
                    carry(i)
                if i > 0:
                    ffn_2(i - 1)
                attention_out(i)
            ffn_turn(NC - 1)
            ffn_1(NC - 1)
            ffn_2(NC - 1)


_INS = ['x', 'L0_tok_W_ve', 'L0_tok_b_ve', 'L0_tok_W_lin', 'L0_tok_b_lin', 'L0_attn_basis',
        'L0_attn_shared_q_w', 'L0_attn_shared_k_w', 'L0_attn_v_coeffs', 'L0_attn_o_coeffs',
        'L0_attn_decay_logits', 'L0_attn_out_scale', 'L0_ffn_W1', 'L0_ffn_b1', 'L0_ffn_W2', 'L0_ffn_b2']


def kernel(**inputs):
    import numpy as _np
    import concourse.bacc as _bacc
    from concourse import mybir as _mybir
    from concourse.bass_utils import run_bass_kernel_spmd as _run

    nc = _bacc.Bacc("TRN2", target_bir_lowering=False, num_devices=1)
    arrays, args = {}, []
    for name in _INS:
        a = _np.ascontiguousarray(inputs[name])
        if a.ndim == 0:
            a = a.reshape(1)
        arrays[f"in_{name}_dram"] = a
        args.append(nc.dram_tensor(f"in_{name}_dram", a.shape, _mybir.dt.from_np(a.dtype), kind="ExternalInput").ap())
    args.append(nc.dram_tensor("out_dram", (B, T, D), _mybir.dt.from_np(_np.dtype("float32")),
                               kind="ExternalOutput").ap())
    build(nc, *args)
    r = _run(nc, [arrays], core_ids=[0])
    return r.results[0]["out_dram"]
```

```python
from contextlib import ExitStack

import concourse.bass as bass
from concourse import mybir

F32 = mybir.dt.float32
F32R = mybir.dt.float32r
ALU = mybir.AluOpType
ACT = mybir.ActivationFunctionType

B, CH, T = 4, 32, 750
D = 128
H, HD = 4, 32
C = 125
NC = T // C
W4 = B * C
STK = 3 * CH + 2
ALPHA = 0.1
EPS_LN = 1e-5
EPS_L2 = 1e-12
LN_MAX = 2.0 ** 63
NBUF = 3
assert NC * C == T and B * CH == 128 and H * HD == D


def build(nc, x, W_ve, b_ve, W_lin, b_lin, basis, wq, wk, v_coeffs, o_coeffs, logits, out_scale,
          W1, b1, W2, b2, out):
    with ExitStack() as ctx:
        def sb(name, shape, dt=F32):
            return ctx.enter_context(nc.sbuf_tensor(name, shape, dt))

        def sem(name):
            return ctx.enter_context(nc.semaphore(name))

        IC = sb("ident_and_centring", [D, 2, D])
        ident, centre = IC[:, 0, :], IC[:, 1, :]
        block_mask = sb("block_mask", [D, H, HD])
        lo_rows = sb("lo_rows", [STK, 1])
        ones_blk = sb("ones_blk", [D, 2, B])
        w_lin = sb("w_lin", [D, D])
        ve_raw = sb("ve_raw", [D, CH + 1])
        VE = sb("ve_stack", [D, STK])
        BL = sb("b_lin_stack", [D, STK])
        wqk = sb("wqk", [D, 2 * D])
        w_basis = sb("w_basis", [D, D])
        w_vc = sb("w_vc", [D, D])
        w_oc = sb("w_oc", [D, D])
        w_1 = sb("w_1", [D, D])
        w_2 = sb("w_2", [D, D])
        b1_col = sb("b1_col", [D, 1])
        b2_row = sb("b2_row", [C, D])
        osc = sb("osc", [D, 1])
        b_lin_col = sb("b_lin_col", [D, 1])
        lin_T = sb("lin_T", [D, 2 * D])
        proj_T = sb("proj_T", [D, 3, STK])
        proj_rep = sb("proj_rep", [D, 3, B, CH])
        basis_ct = sb("basis_ct", [D, STK])
        tr4 = sb("tr4", [D, 4, D])
        w2_T = sb("w2_T", [D, D])
        o_T = sb("o_T", [D, D])
        w_hi = sb("w_hi", [STK, 4 * D], F32R)
        w_stk = sb("w_stk", [STK, 4 * D], F32R)
        Q0, K0, V0, H0 = 0, D, 2 * D, 3 * D
        gram = sb("gram", [D, 3, B, CH])
        gram_lin = sb("gram_lin", [D, 3])
        gram_c = sb("gram_c", [C, 3])

        lg_row = sb("lg_row", [C, H])
        lg_col = sb("lg_col", [D, 1])
        dec_row = sb("dec_row", [C, 4, H])
        dec_col = sb("dec_col", [D, 4])
        key_exp = sb("key_exp", [C, H])
        t_part = sb("t_part", [C, 1])
        t_left = sb("t_left", [D, C])
        t_diff = sb("t_diff", [C, C])
        t_full = sb("t_full", [D, 1])
        key_pow = sb("key_pow", [C, H])
        qry_pow = sb("qry_pow", [D, C])
        chunk_pow = sb("chunk_pow", [D, 1])
        dmask = sb("dmask", [C, H, C])

        xt = sb("xt", [D, T])
        xd = sb("xd", [D, T])
        keep = sb("keep", [D, T])
        last10 = sb("last10", [D, 1])
        s_lr = sb("s_lr", [D, T])
        s_rl = sb("s_rl", [D, T])
        z = sb("z", [D, T])
        z_hi = sb("z_hi", [D, T], F32R)
        z_lo = sb("z_lo", [D, T], F32R)
        z_stk = sb("z_stk", [STK, NC, B, C], F32R)
        quad = sb("quad", [D, 3, T])
        ss = sb("ss", [C, 3, 2, NC // 2 * B])
        rstd = sb("rstd", [C, 2, NC // 2 * B])
        nrm = sb("nrm", [C, 3, 2, NC // 2 * B])
        nrm2 = sb("nrm2", [C, 2, 2, NC // 2 * B])
        rec = sb("rec", [C, 2, 2, NC // 2 * B])
        sc_qk = sb("sc_qk", [C, 2, 2, NC // 2 * B])
        sc_v = sb("sc_v", [C, 2, NC // 2 * B])
        minus_half = sb("minus_half", [C, B])

        def bufs(name, shape):
            return [sb(f"{name}{n}", shape) for n in range(NBUF)]

        h_tok = bufs("h_tok", [C, B, D])
        k_dec = bufs("k_dec", [C, B, D])
        v_sc = bufs("v_sc", [C, B, D])
        qT = bufs("qT", [D, B, C])
        kT = [sb(f"kT{n}", [D, H, B, C]) for n in range(2)]
        q_dec = bufs("q_dec", [D, B, C])
        prob = [sb(f"prob{n}", [C, H, B, C]) for n in range(2)]
        rT = bufs("rT", [D, B, C])
        state = bufs("state", [D, B, D])
        state_m = bufs("state_m", [D, B, D])
        h2 = bufs("h2", [C, B, D])
        h2_b = bufs("h2_b", [C, B, D])
        bn6 = bufs("bn6", [C, B, 6])
        mv = bufs("mv", [C, B, 2])
        ve2 = bufs("ve2", [C, B])
        rstd2 = bufs("rstd2", [C, B])
        xn = bufs("xn", [C, B, D])
        xT = bufs("xT", [D, B, C])
        gT = bufs("gT", [D, B, C])
        y = bufs("y", [C, B, D])

        kv_ps = ctx.enter_context(nc.psum_tensor("kv_ps", [128, 1024], F32))
        hx_ps, qr_ps, kf_ps, f2_ps, s0_ps, s1_ps = (
            ctx.enter_context(nc.psum_tensor(n, [128, 512], F32))
            for n in ("hx_ps", "qr_ps", "kf_ps", "f2_ps", "s0_ps", "s1_ps"))
        st_ps, at_ps = kv_ps[:, 0:512], kv_ps[:, 512:1024]
        sc_ps = [s0_ps, s1_ps]
        gram3 = at_ps[:, 0:3 * STK].rearrange("p (a b) -> p a b", a=3)

        x_in, lin_in, ve_in, bl_in, qk_in, bas_in, vo_in, f_in, row_in, dec_in = (
            sem(n) for n in ("x_in", "lin_in", "ve_in", "bl_in", "qk_in", "bas_in", "vo_in", "f_in",
                             "row_in", "dec_in"))
        pool_c, pool_pw, dv_c = sem("pool_c"), sem("pool_pw"), sem("dv_c")
        ident_ok, centre_ok, bl0_ok, lo_ok, mask_ok, tril_ok, ones_ok = (
            sem(n) for n in ("ident_ok", "centre_ok", "bl0_ok", "lo_ok", "mask_ok", "tril_ok", "ones_ok"))
        b1_in, osc_in, dec_u = sem("b1_in"), sem("osc_in"), sem("dec_u")
        ln_ok, diff_ok, dmask_e, std_ok = sem("ln_ok"), sem("diff_ok"), sem("dmask_e"), sem("std_ok")
        exp_ok, dec_ok, pow_ok, dmask_ok, keypow_ok, half_ok = (
            sem(n) for n in ("exp_ok", "dec_ok", "pow_ok", "dmask_ok", "keypow_ok", "half_ok"))
        ve_ok = sem("ve_ok")
        linT_ps, linT_ok, hrep_ps, projT_ps, projT_ok, qkrep_ps, qkT_ps, qkT_ok = (
            sem(n) for n in ("linT_ps", "linT_ok", "hrep_ps", "projT_ps", "projT_ok", "qkrep_ps",
                             "qkT_ps", "qkT_ok"))
        bct_ps, bct_ok, tr4_ps, tr4_ok, w2T_ps, w2T_ok, vo_ps, oT_ok = (
            sem(n) for n in ("bct_ps", "bct_ok", "tr4_ps", "tr4_ok", "w2T_ps", "w2T_ok", "vo_ps", "oT_ok"))
        rep_ok, kz_ok, whi_h, whi_qk, whi_v = (sem(n) for n in ("rep_ok", "kz_ok", "whi_h", "whi_qk", "whi_v"))
        whi_ok, wstk_ok = sem("whi_ok"), sem("wstk_ok")
        gram_ps, gramc_ps, gram_ok, gramc_ok = (
            sem(n) for n in ("gram_ps", "gramc_ps", "gram_ok", "gramc_ok"))
        z_ok, zhi_ok, zlo_ok, zstk_v, zstk_d, zstk_a, zone_ok = (
            sem(n) for n in ("z_ok", "zhi_ok", "zlo_ok", "zstk_v", "zstk_d", "zstk_a", "zone_ok"))
        quad_ps, quad_ok, ss_ps, ss_ok, pw_ok, scale_ok, stat_v = (
            sem(n) for n in ("quad_ps", "quad_ok", "ss_ps", "ss_ok", "pw_ok", "scale_ok", "stat_v"))
        (qkT_s, qT_ok, kT_ok, kv_s, kd_ok, vs_ok, h_s, h_ok, score_s, prob_ok, qd_ok, rT_s, rT_ok, st_s, st_ok,
         stm_ok, at_s, h2_ok, bn_ok, mv_ok, ve2_ok, rstd2_ok, xn_ok, xT_s, xT_ok, f1_s, gT_ok, h2b_ok, f2_s,
         y_ok) = (
            sem(n) for n in ("qkT_s", "qT_ok", "kT_ok", "kv_s", "kd_ok", "vs_ok", "h_s", "h_ok", "score_s",
                             "prob_ok", "qd_ok", "rT_s", "rT_ok", "st_s", "st_ok", "stm_ok", "at_s", "h2_ok",
                             "bn_ok", "mv_ok", "ve2_ok", "rstd2_ok", "xn_ok", "xT_s", "xT_ok", "f1_s", "gT_ok",
                             "h2b_ok", "f2_s", "y_ok"))
        out_ok = [sem(f"out_ok{n}") for n in range(NBUF)]

        HALF = T // 2
        HC = NC // 2
        quad_bank = {1: [qr_ps, kf_ps, f2_ps], 0: [kf_ps, f2_ps, s0_ps]}
        block = ctx.enter_context(nc.Block())

        @block.sync
        def _(sp):
            sp.dma_start(ve_raw[:, 0:CH], W_ve).then_inc(ve_in, 16)
            sp.dma_start(ve_raw[:, CH:CH + 1], b_ve.unsqueeze(1)).then_inc(ve_in, 16)
            sp.dma_start(wqk[:, 0:D], wq).then_inc(qk_in, 16)
            sp.dma_start(w_basis[:, :], basis).then_inc(bas_in, 16)
            sp.dma_start(w_vc[:, :], v_coeffs).then_inc(vo_in, 16)
            sp.dma_start(w_1[:, :], W1).then_inc(f_in, 16)
            for part, src in enumerate((z_hi, z_lo, z_hi)):
                sp.wait_ge((zhi_ok, zlo_ok, zhi_ok)[part], 1)
                for b in range(B):
                    sp.dma_start(z_stk[part * CH:(part + 1) * CH, 0:NC - 1, b, :].bitcast(F32),
                                 src[CH * b:CH * b + CH, 0:(NC - 1) * C].bitcast(F32)
                                 .rearrange("p (c t) -> p c t", t=C)).then_inc(zstk_d, 16)
            for i in range(NC):
                c = NC - 1 - i
                sp.wait_ge(y_ok, i + 1)
                sp.dma_start(out[:, c * C:(c + 1) * C, :].rearrange("b t f -> t b f"),
                             y[i % NBUF][:, :, :]).then_inc(out_ok[i % NBUF], 16)
            for n in range(NBUF):
                sp.wait_ge(out_ok[n], 16 * (NC // NBUF))

        @block.gpsimd
        def _(pool):
            pool.memset(ident, 0.0).then_inc(pool_c, 1)
            pool.memset(BL[:, :], 0.0).then_inc(bl0_ok, 1)
            pool.wait_ge(pool_c, 1)
            pool.affine_select(out=ident, in_=ident, compare_op=ALU.not_equal, fill=1.0, base=0,
                               pattern=[[-1, D]], channel_multiplier=1).then_inc(ident_ok, 1)
            pool.wait_ge(ident_ok, 1)
            pool.tensor_scalar(centre, ident, -1.0 / D, None, ALU.add).then_inc(centre_ok, 1)
            pool.dma_start(lg_row[:, :], logits.unsqueeze(0).broadcast_to([C, H])).then_inc(dec_in, 16)
            pool.dma_start(lg_col[:, :], logits.unsqueeze(1).unsqueeze(2).broadcast_to([H, HD, 1]))\
                .then_inc(dec_in, 16)
            pool.dma_start(osc[:, :], out_scale.unsqueeze(0).broadcast_to([D, 1])).then_inc(osc_in, 16)
            pool.dma_start(b1_col[:, :], b1.unsqueeze(1)).then_inc(b1_in, 16)
            pool.dma_start(b2_row[:, :], b2.unsqueeze(0).broadcast_to([C, D])).then_inc(row_in, 16)
            pool.wait_ge(bl_in, 16)
            pool.wait_ge(bl0_ok, 1)
            pool.tensor_copy(BL[:, 3 * CH:STK], b_lin_col[:, 0:1].broadcast_to([D, 2])).then_inc(bl0_ok, 1)
            pool.memset(block_mask[:, :, :], 1.0).then_inc(pool_c, 1)
            pool.wait_ge(pool_c, 2)
            pool.affine_select(out=block_mask[:, :, :], in_=block_mask[:, :, :], compare_op=ALU.is_ge, fill=0.0,
                               base=0, pattern=[[-HD, H], [0, HD]], channel_multiplier=1).then_inc(pool_c, 1)
            pool.wait_ge(pool_c, 3)
            pool.affine_select(out=block_mask[:, :, :], in_=block_mask[:, :, :], compare_op=ALU.is_ge, fill=0.0,
                               base=HD - 1, pattern=[[HD, H], [0, HD]], channel_multiplier=-1)\
                .then_inc(mask_ok, 1)
            pool.wait_ge(f_in, 32)
            for w in (w_1, w_2):
                pool.affine_select(out=w[:, :], in_=w[:, :], compare_op=ALU.is_ge, fill=0.0, base=0,
                                   pattern=[[-1, D]], channel_multiplier=1).then_inc(tril_ok, 1)
            pool.wait_ge(tril_ok, 2)
            pool.memset(z_stk[3 * CH:STK, :, :, :].bitcast(F32), 1.0).then_inc(zone_ok, 1)
            pool.wait_ge(zone_ok, 1)
            pool.memset(kT[0][:, :, :, :], 0.0).then_inc(kz_ok, 1)
            pool.wait_ge(mask_ok, 1)
            pool.tensor_copy(ones_blk[:, 1, :], block_mask[:, :, 0]).then_inc(ones_ok, 1)
            pool.tensor_scalar(ones_blk[:, 0, :], block_mask[:, :, 0], 1.0 / D, None, ALU.mult)\
                .then_inc(ones_ok, 1)
            pool.iota(t_diff[:, :], pattern=[[-1, C]], base=-1, channel_multiplier=1,
                      allow_small_or_imprecise_dtypes=True).then_inc(pool_pw, 1)
            pool.iota(t_part[:, :], pattern=[[0, 1]], base=0, channel_multiplier=1,
                      allow_small_or_imprecise_dtypes=True).then_inc(pool_pw, 1)
            pool.iota(t_left[:, :], pattern=[[-1, C]], base=C - 1, channel_multiplier=0,
                      allow_small_or_imprecise_dtypes=True).then_inc(pool_pw, 1)
            pool.memset(t_full[:, :], float(C)).then_inc(pool_pw, 1)
            pool.memset(minus_half[:, :], -0.5).then_inc(half_ok, 1)
            pool.wait_ge(pool_pw, 4)
            pool.tensor_scalar(t_diff[:, :], t_diff[:, :], 0.0, None, ALU.max).then_inc(diff_ok, 1)
            pool.memset(kT[1][:, :, :, :], 0.0).then_inc(kz_ok, 1)
            pool.wait_ge(dmask_e, 1)
            pool.affine_select(out=dmask[:, :, :], in_=dmask[:, :, :], compare_op=ALU.is_ge, fill=0.0, base=-1,
                               pattern=[[0, H], [-1, C]], channel_multiplier=1).then_inc(dmask_ok, 1)
            for i in range(NC):
                n = i % NBUF
                if i > 0:
                    pool.wait_ge(qT_ok, i + 1)
                    pool.wait_ge(pow_ok, 2)
                    if i > NBUF:
                        pool.wait_ge(rT_s, i - NBUF + 1)
                    pool.tensor_tensor(q_dec[n][:, :, :], qT[n][:, :, :],
                                       qry_pow[:, :].unsqueeze(1).broadcast_to([D, B, C]),
                                       ALU.mult).then_inc(qd_ok, 1)
                if i < NC - 1:
                    pool.wait_ge(st_ok, i + 1)
                    if i >= NBUF:
                        pool.wait_ge(rT_s, i - NBUF + 2)
                    pool.tensor_tensor(state_m[n][:, :, :], state[n][:, :, :],
                                       block_mask[:, :, :].rearrange("p h d -> p (h d)").unsqueeze(1)
                                       .broadcast_to([D, B, D]), ALU.mult).then_inc(stm_ok, 1)
                pool.wait_ge(mv_ok, B * (i + 1))
                pool.tensor_scalar(ve2[n][:, :], mv[n][:, :, 1], EPS_LN, None, ALU.add).then_inc(ve2_ok, 1)
                pool.wait_ge(ve2_ok, i + 1)
                pool.wait_ge(half_ok, 1)
                pool.tensor_tensor(rstd2[n][:, :], ve2[n][:, :], minus_half[:, :], ALU.pow)\
                    .then_inc(rstd2_ok, 1)
                pool.wait_ge(row_in, 16)
                if i >= NBUF:
                    pool.wait_ge(y_ok, i - NBUF + 1)
                pool.tensor_tensor(h2_b[n][:, :, :], h2[n][:, :, :],
                                   b2_row[:, :].unsqueeze(1).broadcast_to([C, B, D]), ALU.add)\
                    .then_inc(h2b_ok, 1)

        @block.scalar
        def _(act):
            act.dma_start(w_lin[:, :], W_lin).then_inc(lin_in, 16)
            act.dma_start(b_lin_col[:, 0:1], b_lin.unsqueeze(1)).then_inc(bl_in, 16)
            act.dma_start(xt[:, :], x.rearrange("b c t -> (b c) t")).then_inc(x_in, 16)
            act.dma_start(wqk[:, D:2 * D], wk).then_inc(qk_in, 16)
            act.dma_start(w_oc[:, :], o_coeffs).then_inc(vo_in, 16)
            act.dma_start(w_2[:, :], W2).then_inc(f_in, 16)
            act.wait_ge(linT_ps, 1)
            act.activation(lin_T[:, :], kv_ps[:, 0:2 * D], ACT.Copy).then_inc(linT_ok, 1)
            act.wait_ge(projT_ps, 1)
            act.activation(proj_T[:, 0, :], hx_ps[:, 0:STK], ACT.Copy).then_inc(projT_ok, 1)
            act.wait_ge(hrep_ps, 1)
            act.activation(w_hi[:, H0:H0 + D], s1_ps[0:STK, 0:D], ACT.Copy).then_inc(whi_h, 1)
            act.wait_ge(qkrep_ps, 1)
            act.activation(w_hi[:, Q0:V0], qr_ps[0:STK, 0:2 * D], ACT.Copy).then_inc(whi_qk, 1)
            act.wait_ge(bct_ps, 1)
            act.activation(basis_ct[:, :], f2_ps[:, 0:STK], ACT.Copy).then_inc(bct_ok, 1)
            act.wait_ge(tr4_ps, 1)
            act.activation(tr4[:, :, :].rearrange("p a b -> p (a b)"), s0_ps[:, :], ACT.Copy)\
                .then_inc(tr4_ok, 1)
            act.wait_ge(vo_ps, 1)
            act.activation(w_hi[:, V0:H0], f2_ps[0:STK, 0:D], ACT.Copy).then_inc(whi_v, 1)
            act.wait_ge(zhi_ok, 1)
            for b in range(B):
                act.activation(z_stk[2 * CH:3 * CH, NC - 1, b, :],
                               z_hi[CH * b:CH * b + CH, (NC - 1) * C:T].bitcast(F32), ACT.Copy)\
                    .then_inc(zstk_a, 1)
            act.wait_ge(vo_ps, 2)
            act.wait_ge(osc_in, 16)
            act.activation(o_T[:, :], kv_ps[:, 0:D], ACT.Copy, scale=osc[:, 0:1]).then_inc(oT_ok, 1)
            act.wait_ge(w2T_ps, 1)
            act.activation(w2_T[:, :], s0_ps[:, 0:D], ACT.Copy).then_inc(w2T_ok, 1)

            def q_out(i):
                act.wait_ge(qkT_s, 2 * i + 1)
                if i >= NBUF:
                    act.wait_ge(qd_ok, i - NBUF)
                    act.wait_ge(score_s, H * (i - NBUF + 1))
                act.activation(qT[i % NBUF][:, :, :].rearrange("p b t -> p (b t)"), qr_ps[:, 0:W4], ACT.Copy)\
                    .then_inc(qT_ok, 1)

            def k_out(i):
                act.wait_ge(qkT_s, 2 * i + 2)
                if i < 2:
                    act.wait_ge(kz_ok, i + 1)
                else:
                    act.wait_ge(score_s, H * (i - 1))
                for h in range(H):
                    rows = slice(h * HD, (h + 1) * HD)
                    act.activation(kT[i % 2][rows, h, :, :].rearrange("p b t -> p (b t)"), kf_ps[rows, 0:W4],
                                   ACT.Copy).then_inc(kT_ok, 1)

            def h_out(i):
                act.wait_ge(h_s, i + 1)
                if i >= NBUF:
                    act.wait_ge(h2_ok, B * (i - NBUF + 1))
                act.activation(h_tok[i % NBUF][:, :, :].rearrange("p b f -> p (b f)"), hx_ps[0:C, :], ACT.Copy)\
                    .then_inc(h_ok, 1)

            def r_out(i):
                act.wait_ge(rT_s, i + 1)
                if i >= NBUF:
                    act.wait_ge(at_s, i - NBUF + 1)
                act.activation(rT[i % NBUF][:, :, :].rearrange("p b t -> p (b t)"), qr_ps[:, 0:W4], ACT.Copy)\
                    .then_inc(rT_ok, 1)

            def ffn_in(i):
                act.wait_ge(xT_s, i + 1)
                if i >= NBUF:
                    act.wait_ge(f1_s, i - NBUF + 1)
                act.activation(xT[i % NBUF][:, :, :].rearrange("p b t -> p (b t)"), hx_ps[:, 0:W4], ACT.Copy)\
                    .then_inc(xT_ok, 1)

            def ffn_gelu(i):
                act.wait_ge(f1_s, i + 1)
                if i == 0:
                    act.wait_ge(b1_in, 16)
                if i >= NBUF:
                    act.wait_ge(f2_s, i - NBUF + 1)
                act.activation(gT[i % NBUF][:, :, :].rearrange("p b t -> p (b t)"), kf_ps[:, 0:W4], ACT.Gelu,
                               bias=b1_col[:, 0:1]).then_inc(gT_ok, 1)

            def roots(half):
                act.wait_ge(ss_ok, 3 * (2 - half))
                act.activation(nrm[:, :, half, :], ss[:, :, half, :], ACT.Sqrt).then_inc(pw_ok, 1)

            act.wait_ge(dec_in, 32)
            act.activation(dec_row[:, 0, :], lg_row[:, :], ACT.Exp, scale=-1.0).then_inc(exp_ok, 1)
            act.activation(dec_col[:, 0:1], lg_col[:, :], ACT.Exp, scale=-1.0).then_inc(exp_ok, 1)
            q_out(0)
            k_out(0)
            act.wait_ge(dec_u, 2)
            act.activation(dec_row[:, 2, :], dec_row[:, 1, :], ACT.Ln).then_inc(ln_ok, 1)
            act.activation(dec_col[:, 2:3], dec_col[:, 1:2], ACT.Ln).then_inc(ln_ok, 1)
            h_out(0)
            act.wait_ge(dec_ok, 3)
            act.wait_ge(diff_ok, 1)
            for h in range(H):
                ins = act.activation(dmask[:, h, :], t_diff[:, :], ACT.Exp, scale=dec_row[:, 3, h:h + 1])
            ins.then_inc(dmask_e, 1)
            act.activation(key_pow[:, :], key_exp[:, :], ACT.Exp).then_inc(keypow_ok, 1)
            act.activation(qry_pow[:, :], t_left[:, :], ACT.Exp, scale=dec_col[:, 3:4]).then_inc(pow_ok, 1)
            act.activation(chunk_pow[:, :], t_full[:, :], ACT.Exp, scale=dec_col[:, 3:4]).then_inc(pow_ok, 1)
            roots(1)
            r_out(0)
            roots(0)
            for i in range(1, NC):
                q_out(i)
                k_out(i)
                h_out(i)
                ffn_in(i - 1)
                r_out(i)
                ffn_gelu(i - 1)
            ffn_in(NC - 1)
            ffn_gelu(NC - 1)

        @block.vector
        def _(dve):
            dve.memset(xd[:, 0:1], 0.0).then_inc(dv_c, 1)
            dve.memset(lo_rows[:, :], 0.0).then_inc(lo_ok, 1)
            dve.wait_ge(lo_ok, 1)
            dve.memset(lo_rows[2 * CH:3 * CH, :], -1.0).then_inc(lo_ok, 1)
            dve.memset(keep[:, :], 1.0 - ALPHA).then_inc(dv_c, 1)
            dve.wait_ge(ident_ok, 1)
            dve.tensor_scalar(lo_rows[3 * CH:STK, :], ident[3 * CH:STK, STK - 1:STK], -1.0, None, ALU.mult)\
                .then_inc(lo_ok, 1)
            dve.wait_ge(ve_in, 32)
            dve.tensor_scalar(VE[:, 0:3 * CH].rearrange("p (a c) -> p a c", a=3),
                              ve_raw[:, 0:CH].unsqueeze(1).broadcast_to([D, 3, CH]), 0.5 * ALPHA, None,
                              ALU.mult).then_inc(ve_ok, 1)
            dve.tensor_copy(VE[:, 3 * CH:STK], ve_raw[:, CH:CH + 1].broadcast_to([D, 2])).then_inc(ve_ok, 1)
            dve.wait_ge(x_in, 16)
            dve.tensor_tensor(xd[:, 1:T], xt[:, 1:T], xt[:, 0:T - 1], ALU.subtract).then_inc(dv_c, 1)
            dve.wait_ge(dv_c, 3)
            dve.tensor_scalar(last10[:, :], xd[:, T - 1:T], 1.0 / ALPHA, None, ALU.mult).then_inc(dv_c, 1)
            dve.tensor_tensor_scan(s_lr[:, :], keep[:, :], xd[:, :], 0.0, ALU.mult, ALU.add).then_inc(dv_c, 1)
            dve.wait_ge(dv_c, 4)
            dve.tensor_tensor_scan(s_rl[:, ::-1], keep[:, :], xd[:, ::-1], last10[:, 0:1], ALU.mult,
                                   ALU.add).then_inc(dv_c, 1)
            dve.wait_ge(dv_c, 6)
            dve.tensor_tensor(z[:, :], s_lr[:, :], s_rl[:, :], ALU.add).then_inc(z_ok, 1)
            dve.wait_ge(z_ok, 1)
            dve.tensor_copy(z_hi[:, :], z[:, :]).then_inc(zhi_ok, 1)
            dve.wait_ge(zhi_ok, 1)
            dve.tensor_tensor(z_lo[:, :], z[:, :], z_hi[:, :].bitcast(F32), ALU.subtract).then_inc(zlo_ok, 1)
            for part, src in ((0, z_hi), (1, z_lo)):
                dve.wait_ge((zhi_ok, zlo_ok)[part], 1)
                for b in range(B):
                    dve.tensor_copy(z_stk[part * CH:(part + 1) * CH, NC - 1, b, :],
                                    src[CH * b:CH * b + CH, (NC - 1) * C:T].bitcast(F32)).then_inc(zstk_v, 1)

            def stack_w(ps, c0, c1, hi_ok):
                dve.wait_ge(hi_ok, 1)
                dve.scalar_tensor_tensor(out=w_stk[:, c0:c1], in0=w_hi[:, c0:c1].bitcast(F32),
                                         scalar=lo_rows[:, 0:1], in1=ps, op0=ALU.mult, op1=ALU.add)\
                    .then_inc(wstk_ok, 1)
            dve.wait_ge(lo_ok, 3)
            stack_w(qr_ps[0:STK, 0:2 * D], Q0, V0, whi_qk)
            stack_w(s1_ps[0:STK, 0:D], H0, H0 + D, whi_h)
            dve.wait_ge(exp_ok, 2)
            dve.tensor_scalar(dec_row[:, 1, :], dec_row[:, 0, :], 1.0, LN_MAX, ALU.add, ALU.min).then_inc(dec_u, 1)
            dve.tensor_scalar(dec_col[:, 1:2], dec_col[:, 0:1], 1.0, LN_MAX, ALU.add, ALU.min).then_inc(dec_u, 1)
            dve.wait_ge(qkT_ps, 1)
            dve.tensor_copy(proj_T[:, 1:3, :].rearrange("p a b -> p (a b)"), kf_ps[:, 0:2 * STK])\
                .then_inc(qkT_ok, 1)
            dve.wait_ge(qkT_ok, 1)
            dve.wait_ge(projT_ok, 1)
            dve.tensor_copy(proj_rep[:, :, :, :], proj_T[:, :, 0:CH].unsqueeze(2).broadcast_to([D, 3, B, CH]))\
                .then_inc(rep_ok, 1)
            stack_w(f2_ps[0:STK, 0:D], V0, H0, whi_v)
            dve.wait_ge(ln_ok, 2)
            dve.tensor_scalar(dec_row[:, 3, :], dec_row[:, 2, :], -1.0, None, ALU.mult).then_inc(dec_ok, 1)
            dve.tensor_scalar(dec_col[:, 3:4], dec_col[:, 2:3], -1.0, None, ALU.mult).then_inc(dec_ok, 1)
            dve.wait_ge(pool_pw, 4)
            dve.tensor_scalar(key_exp[:, :], dec_row[:, 2, :], t_part[:, 0:1], -1.0, ALU.mult, ALU.mult)\
                .then_inc(dec_ok, 1)
            dve.wait_ge(gram_ps, 1)
            dve.wait_ge(mask_ok, 1)
            for a in range(3):
                dve.tensor_tensor(gram[:, a, :, :], gram3[:, a, 0:CH].unsqueeze(1).broadcast_to([D, B, CH]),
                                  block_mask[:, :, :], ALU.mult).then_inc(gram_ok, 1)
            dve.tensor_scalar(gram_lin[:, :], gram3[:, :, 3 * CH], 2.0, None, ALU.mult).then_inc(gram_ok, 1)
            dve.tensor_scalar(gram_c[:, 0:1], at_ps[0:C, 3 * STK:3 * STK + 1], 1.0 / D, EPS_LN, ALU.mult, ALU.add)\
                .then_inc(gram_ok, 1)
            dve.tensor_copy(gram_c[:, 1:3], at_ps[0:C, 3 * STK + 1:3 * STK + 3]).then_inc(gram_ok, 1)

            def quads(half):
                first = 3 * (1 - half)
                for a in range(3):
                    dve.wait_ge(quad_ps, first + a + 1)
                    dve.scalar_tensor_tensor(out=quad[:, a, half * HALF:(half + 1) * HALF],
                                             in0=quad_bank[half][a][:, 0:HALF], scalar=gram_lin[:, a:a + 1],
                                             in1=z[:, half * HALF:(half + 1) * HALF], op0=ALU.add,
                                             op1=ALU.mult).then_inc(quad_ok, 1)

            def sums(half):
                dve.wait_ge(ss_ps, 2 - half)
                for a in range(3):
                    at = (half * 3 + a) * HC * B
                    dve.tensor_scalar(ss[:, a, half, :], hx_ps[0:C, at:at + HC * B], gram_c[:, a:a + 1],
                                      EPS_LN if a == 0 else 0.0, ALU.add, ALU.max).then_inc(ss_ok, 1)

            def scales(half):
                k = 5 * (1 - half)
                dve.wait_ge(pw_ok, 2 - half)
                dve.reciprocal(rstd[:, half, :], nrm[:, 0, half, :]).then_inc(stat_v, 1)
                dve.wait_ge(stat_v, k + 1)
                rb = rstd[:, half, :].unsqueeze(1).broadcast_to([C, 2, HC * B])
                dve.tensor_tensor(nrm2[:, :, half, :], nrm[:, 1:3, half, :], rb, ALU.mult).then_inc(stat_v, 1)
                dve.wait_ge(stat_v, k + 2)
                dve.tensor_scalar(nrm2[:, :, half, :], nrm2[:, :, half, :], EPS_L2, None, ALU.max)\
                    .then_inc(stat_v, 1)
                dve.wait_ge(stat_v, k + 3)
                dve.reciprocal(rec[:, :, half, :], nrm2[:, :, half, :]).then_inc(stat_v, 1)
                dve.wait_ge(stat_v, k + 4)
                dve.tensor_tensor(sc_qk[:, :, half, :], rec[:, :, half, :], rb, ALU.mult).then_inc(stat_v, 1)
                dve.wait_ge(stat_v, k + 5)
                dve.tensor_tensor(sc_v[:, half, :], sc_qk[:, 1, half, :], rstd[:, half, :], ALU.mult)\
                    .then_inc(scale_ok, 1)

            kv = kv_ps[0:C, :].rearrange("p (b f) -> p b f", b=B)

            def probs(i, h):
                if h == 0 and i == 0:
                    dve.wait_ge(dmask_ok, 1)
                if h == 0 and i >= 2:
                    dve.wait_ge(rT_s, i - 1)
                dve.wait_ge(score_s, H * i + h + 1)
                dve.tensor_tensor(prob[i % 2][:, h, :, :],
                                  sc_ps[h % 2][0:C, 0:W4].rearrange("p (b t) -> p b t", b=B),
                                  dmask[:, h, :].unsqueeze(1).broadcast_to([C, B, C]), ALU.mult)\
                    .then_inc(prob_ok, 1)

            def keys(i):
                n = i % NBUF
                dve.wait_ge(kv_s, 2 * i + 2)
                if i == 0:
                    dve.wait_ge(keypow_ok, 1)
                if i >= NBUF:
                    dve.wait_ge(st_s, i - NBUF + 1)
                dve.tensor_tensor(k_dec[n][:, :, :].rearrange("p b (h d) -> p b h d", h=H),
                                  kv[:, :, 0:D].rearrange("p b (h d) -> p b h d", h=H),
                                  key_pow[:, :].unsqueeze(1).unsqueeze(3).broadcast_to([C, B, H, HD]),
                                  ALU.mult).then_inc(kd_ok, 1)

            def values(i):
                n, c = i % NBUF, NC - 1 - i
                dve.wait_ge(kv_s, 2 * i + 2)
                dve.wait_ge(scale_ok, 1 if c >= HC else 2)
                if i >= NBUF:
                    dve.wait_ge(rT_s, i - NBUF + 1)
                dve.tensor_tensor(v_sc[n][:, :, :], kv[:, :, D:2 * D],
                                  sc_v[:, c // HC, (c % HC) * B:(c % HC) * B + B].unsqueeze(2)
                                  .broadcast_to([C, B, D]), ALU.mult).then_inc(vs_ok, 1)

            def carry_on(i):
                dve.wait_ge(st_s, i + 1)
                new = state[i % NBUF][:, :, :].rearrange("p b f -> p (b f)")
                if i >= NBUF:
                    dve.wait_ge(stm_ok, i - NBUF + 1)
                if i == 0:
                    dve.tensor_copy(new, st_ps).then_inc(st_ok, 1)
                else:
                    dve.wait_ge(st_ok, i)
                    dve.wait_ge(pow_ok, 2)
                    dve.scalar_tensor_tensor(
                        out=new, in0=state[(i - 1) % NBUF][:, :, :].rearrange("p b f -> p (b f)"),
                        scalar=chunk_pow[:, 0:1], in1=st_ps, op0=ALU.mult, op1=ALU.add).then_inc(st_ok, 1)

            def last_sum(i):
                n = i % NBUF
                dve.wait_ge(f2_s, i + 1)
                dve.wait_ge(h2b_ok, i + 1)
                if i >= NBUF:
                    dve.wait_ge(out_ok[n], 16 * (i // NBUF))
                dve.tensor_tensor(y[n][:, :, :], f2_ps[0:C, :].rearrange("p (b f) -> p b f", b=B),
                                  h2_b[n][:, :, :], ALU.add).then_inc(y_ok, 1)

            def residual(i):
                n, c = i % NBUF, NC - 1 - i
                dve.wait_ge(at_s, i + 1)
                dve.wait_ge(h_ok, i + 1)
                if i >= NBUF:
                    dve.wait_ge(h2b_ok, i - NBUF + 1)
                for b in range(B):
                    at = (c % HC) * B + b
                    dve.scalar_tensor_tensor(out=h2[n][:, b, :], in0=at_ps[0:C, b * D:(b + 1) * D],
                                             scalar=sc_qk[:, 0, c // HC, at:at + 1],
                                             in1=h_tok[n][:, b, :], op0=ALU.mult, op1=ALU.add)\
                        .then_inc(h2_ok, 1)
                for b in range(B):
                    dve.wait_ge(h2_ok, B * i + b + 1)
                    dve.bn_stats(bn6[n][:, b, :], h2[n][:, b, :]).then_inc(bn_ok, 1)
                for b in range(B):
                    dve.wait_ge(bn_ok, B * i + b + 1)
                    dve.bn_aggr(mv[n][:, b, :], bn6[n][:, b, :]).then_inc(mv_ok, 1)

            def normed(i):
                n = i % NBUF
                dve.wait_ge(rstd2_ok, i + 1)
                if i >= NBUF:
                    dve.wait_ge(xT_s, i - NBUF + 1)
                for b in range(B):
                    dve.tensor_scalar(xn[n][:, b, :], h2[n][:, b, :], mv[n][:, b, 0:1], rstd2[n][:, b:b + 1],
                                      ALU.subtract, ALU.mult).then_inc(xn_ok, 1)

            quads(1)
            probs(0, 0)
            probs(0, 1)
            keys(0)
            sums(1)
            probs(0, 2)
            scales(1)
            values(0)
            probs(0, 3)
            quads(0)
            carry_on(0)
            sums(0)
            residual(0)
            scales(0)
            for i in range(1, NC):
                probs(i, 0)
                probs(i, 1)
                if i < NC - 1:
                    keys(i)
                values(i)
                probs(i, 2)
                normed(i - 1)
                probs(i, 3)
                if i < NC - 1:
                    carry_on(i)
                last_sum(i - 1)
                residual(i)
            normed(NC - 1)
            last_sum(NC - 1)

        @block.tensor
        def _(pe):
            pe.wait_ge(lin_in, 16)
            pe.wait_ge(centre_ok, 1)
            pe.matmul(kv_ps[:, 0:2 * D], w_lin[:, :], IC[:, :, :].rearrange("p a b -> p (a b)"),
                      start=True, stop=True).then_inc(linT_ps, 1)
            pe.wait_ge(linT_ok, 1)
            pe.wait_ge(ve_ok, 2)
            pe.wait_ge(bl0_ok, 2)
            pe.matmul(hx_ps[:, 0:STK], lin_T[:, D:2 * D], VE[:, :], start=True, stop=False)
            pe.matmul(hx_ps[:, 0:STK], centre, BL[:, :], start=False, stop=True).then_inc(projT_ps, 1)
            pe.matmul(s1_ps[0:STK, 0:D], VE[:, :], lin_T[:, 0:D], start=True, stop=False)
            pe.matmul(s1_ps[0:STK, 0:D], BL[:, :], ident, start=False, stop=True).then_inc(hrep_ps, 1)
            pe.wait_ge(projT_ok, 1)
            pe.wait_ge(qk_in, 32)
            pe.matmul(qr_ps[0:STK, 0:2 * D], proj_T[:, 0, :], wqk[:, :], start=True, stop=True)\
                .then_inc(qkrep_ps, 1)
            pe.wait_ge(bas_in, 16)
            pe.matmul(f2_ps[:, 0:STK], w_basis[:, :], proj_T[:, 0, :], start=True, stop=True)\
                .then_inc(bct_ps, 1)
            pe.matmul(kf_ps[:, 0:STK], wqk[:, 0:D], proj_T[:, 0, :], start=True, stop=True)
            pe.matmul(kf_ps[:, STK:2 * STK], wqk[:, D:2 * D], proj_T[:, 0, :], start=True, stop=True)\
                .then_inc(qkT_ps, 1)
            pe.wait_ge(vo_in, 32)
            pe.wait_ge(tril_ok, 2)
            for j, w in enumerate((w_vc, w_oc, w_basis, w_1)):
                ins = pe.transpose(s0_ps[:, j * D:(j + 1) * D], w[:, :], ident)
            ins.then_inc(tr4_ps, 1)
            pe.wait_ge(tr4_ok, 1)
            pe.wait_ge(bct_ok, 1)
            pe.matmul(f2_ps[0:STK, 0:D], basis_ct[:, :], tr4[:, 0, :], start=True, stop=True)\
                .then_inc(vo_ps, 1)
            pe.matmul(kv_ps[:, 0:D], tr4[:, 1, :], tr4[:, 2, :], start=True, stop=True).then_inc(vo_ps, 1)
            pe.transpose(s0_ps[:, 0:D], w_2[:, :], ident).then_inc(w2T_ps, 1)

            def forms():
                pe.wait_ge(rep_ok, 1)
                for a in range(3):
                    pe.matmul(at_ps[:, a * STK:(a + 1) * STK], proj_rep[:, a, :, :].rearrange("p b c -> p (b c)"),
                              proj_T[:, a, :], start=True, stop=True)
                for a in range(3):
                    ins = pe.matmul(at_ps[0:C, 3 * STK + a:3 * STK + a + 1],
                                    proj_T[:, a, 3 * CH:3 * CH + 1].broadcast_to([D, C]),
                                    proj_T[:, a, 3 * CH:3 * CH + 1], start=True, stop=True)
                ins.then_inc(gram_ps, 1)

            def quads(half):
                if half == 1:
                    pe.wait_ge(gram_ok, 6)
                    pe.wait_ge(qT_ok, 1)
                    pe.wait_ge(kT_ok, H)
                    pe.wait_ge(wstk_ok, 3)
                else:
                    pe.wait_ge(prob_ok, 3)
                    pe.wait_ge(quad_ok, 3)
                for a in range(3):
                    pe.matmul(quad_bank[half][a][:, 0:HALF], gram[:, a, :, :].rearrange("p b c -> p (b c)"),
                              z[:, half * HALF:(half + 1) * HALF], start=True, stop=True).then_inc(quad_ps, 1)

            def sums(half):
                if half == 1:
                    pe.wait_ge(ones_ok, 2)
                    pe.wait_ge(h_ok, 1)
                else:
                    pe.wait_ge(ss_ok, 3)
                for a in range(3):
                    pe.wait_ge(quad_ok, 3 * (1 - half) + a + 1)
                    for c in range(HC):
                        at = ((half * 3 + a) * HC + c) * B
                        first = half * HALF + c * C
                        ins = pe.matmul(hx_ps[0:C, at:at + B], quad[:, a, first:first + C],
                                        ones_blk[:, min(a, 1), :], start=True, stop=True)
                ins.then_inc(ss_ps, 1)

            def project_qk(i):
                c = NC - 1 - i
                zc = z_stk[:, c, :, :].rearrange("p b t -> p (b t)")
                if i > 0:
                    pe.wait_ge(rT_ok, i)
                pe.matmul(qr_ps[:, 0:W4], w_stk[:, Q0:Q0 + D], zc, start=True, stop=True).then_inc(qkT_s, 1)
                if i == 0:
                    pe.wait_ge(qkT_ok, 1)
                if i > 1:
                    pe.wait_ge(gT_ok, i - 1)
                pe.matmul(kf_ps[:, 0:W4], w_stk[:, K0:K0 + D], zc, start=True, stop=True).then_inc(qkT_s, 1)

            def project_kv(i):
                c = NC - 1 - i
                if i == 0:
                    pe.wait_ge(oT_ok, 1)
                    pe.wait_ge(wstk_ok, 3)
                else:
                    pe.wait_ge(st_ok, i)
                for b in range(B):
                    if b == 2 and i == 0:
                        pe.wait_ge(gram_ok, 6)
                    if b == 2 and i > 0:
                        pe.wait_ge(h2_ok, B * i)
                    ins = pe.matmul(kv_ps[0:C, b * 2 * D:(b + 1) * 2 * D], z_stk[:, c, b, :],
                                    w_stk[:, K0:K0 + 2 * D], start=True, stop=True)
                    if b % 2:
                        ins.then_inc(kv_s, 1)

            def project_h(i):
                c = NC - 1 - i
                if i == 1:
                    pe.wait_ge(ss_ok, 6)
                if i > 1:
                    pe.wait_ge(xT_ok, i - 1)
                for b in range(B):
                    ins = pe.matmul(hx_ps[0:C, b * D:(b + 1) * D], z_stk[:, c, b, :],
                                    w_stk[:, H0:H0 + D], start=True, stop=True)
                ins.then_inc(h_s, 1)

            def score(i, h):
                if h == 0:
                    pe.wait_ge(qT_ok, i + 1)
                    if i == 0:
                        pe.wait_ge(w2T_ok, 1)
                pe.wait_ge(kT_ok, H * i + h + 1)
                if H * i + h >= 2:
                    pe.wait_ge(prob_ok, H * i + h - 1)
                for b in range(B):
                    ins = pe.matmul(sc_ps[h % 2][0:C, b * C:(b + 1) * C], kT[i % 2][:, h, b, :],
                                    qT[i % NBUF][:, b, :], start=True, stop=True)
                ins.then_inc(score_s, 1)

            def retrieve(i):
                n = i % NBUF
                if i > 0:
                    pe.wait_ge(qd_ok, i)
                    pe.wait_ge(stm_ok, i)
                    for b in range(B):
                        pe.matmul(qr_ps[:, b * C:(b + 1) * C], state_m[(i - 1) % NBUF][:, b, :],
                                  q_dec[n][:, b, :], start=(b == 0), stop=False, skip_group_check=True)
                pe.wait_ge(vs_ok, i + 1)
                for b in range(B):
                    if b == 0:
                        pe.wait_ge(prob_ok, H * (i + 1))
                    for h in range(H):
                        cols = slice(h * HD, (h + 1) * HD)
                        ins = pe.matmul(qr_ps[cols, b * C:(b + 1) * C], v_sc[n][:, b, cols],
                                        prob[i % 2][:, h, b, :], start=(i == 0 and b == 0),
                                        stop=(b == B - 1), skip_group_check=True)
                ins.then_inc(rT_s, 1)

            def carry(i):
                n = i % NBUF
                pe.wait_ge(kd_ok, i + 1)
                pe.wait_ge(vs_ok, i + 1)
                for b in range(B):
                    ins = pe.matmul(st_ps[:, b * D:(b + 1) * D], k_dec[n][:, b, :], v_sc[n][:, b, :],
                                    start=True, stop=True)
                ins.then_inc(st_s, 1)

            def attention_out(i):
                n = i % NBUF
                pe.wait_ge(rT_ok, i + 1)
                for b in range(B):
                    ins = pe.matmul(at_ps[0:C, b * D:(b + 1) * D], rT[n][:, b, :], o_T[:, :],
                                    start=True, stop=True)
                ins.then_inc(at_s, 1)

            def ffn_turn(i):
                n = i % NBUF
                pe.wait_ge(h_ok, min(i + 2, NC))
                for b in range(B):
                    pe.wait_ge(xn_ok, B * i + b + 1)
                    ins = pe.transpose(hx_ps[:, b * C:(b + 1) * C], xn[n][:, b, :], ident[0:C, 0:C])
                ins.then_inc(xT_s, 1)

            def ffn_1(i):
                pe.wait_ge(xT_ok, i + 1)
                pe.matmul(kf_ps[:, 0:W4], tr4[:, 3, :], xT[i % NBUF][:, :, :].rearrange("p b t -> p (b t)"),
                          start=True, stop=True).then_inc(f1_s, 1)

            def ffn_2(i):
                n = i % NBUF
                pe.wait_ge(gT_ok, i + 1)
                if i > 0:
                    pe.wait_ge(y_ok, i)
                for b in range(B):
                    ins = pe.matmul(f2_ps[0:C, b * D:(b + 1) * D], gT[n][:, b, :], w2_T[:, :],
                                    start=True, stop=True)
                ins.then_inc(f2_s, 1)

            pe.wait_ge(wstk_ok, 2)
            pe.wait_ge(zone_ok, 1)
            pe.wait_ge(zstk_v, 2 * B)
            pe.wait_ge(zstk_a, B)
            project_qk(0)
            project_h(0)
            forms()
            quads(1)
            score(0, 0)
            score(0, 1)
            project_kv(0)
            sums(1)
            score(0, 2)
            score(0, 3)
            retrieve(0)
            quads(0)
            carry(0)
            attention_out(0)
            sums(0)
            pe.wait_ge(zstk_d, 16 * 3 * B)
            for i in range(1, NC):
                project_qk(i)
                project_h(i)
                score(i, 0)
                score(i, 1)
                project_kv(i)
                score(i, 2)
                score(i, 3)
                ffn_turn(i - 1)
                ffn_1(i - 1)
                retrieve(i)
                if i < NC - 1:
                    carry(i)
                ffn_2(i - 1)
                attention_out(i)
            ffn_turn(NC - 1)
            ffn_1(NC - 1)
            ffn_2(NC - 1)


_INS = ['x', 'L0_tok_W_ve', 'L0_tok_b_ve', 'L0_tok_W_lin', 'L0_tok_b_lin', 'L0_attn_basis',
        'L0_attn_shared_q_w', 'L0_attn_shared_k_w', 'L0_attn_v_coeffs', 'L0_attn_o_coeffs',
        'L0_attn_decay_logits', 'L0_attn_out_scale', 'L0_ffn_W1', 'L0_ffn_b1', 'L0_ffn_W2', 'L0_ffn_b2']


def kernel(**inputs):
    import numpy as _np
    import concourse.bacc as _bacc
    from concourse import mybir as _mybir
    from concourse.bass_utils import run_bass_kernel_spmd as _run

    nc = _bacc.Bacc("TRN2", target_bir_lowering=False, num_devices=1)
    arrays, args = {}, []
    for name in _INS:
        a = _np.ascontiguousarray(inputs[name])
        if a.ndim == 0:
            a = a.reshape(1)
        arrays[f"in_{name}_dram"] = a
        args.append(nc.dram_tensor(f"in_{name}_dram", a.shape, _mybir.dt.from_np(a.dtype), kind="ExternalInput").ap())
    args.append(nc.dram_tensor("out_dram", (B, T, D), _mybir.dt.from_np(_np.dtype("float32")),
                               kind="ExternalOutput").ap())
    build(nc, *args)
    r = _run(nc, [arrays], core_ids=[0])
    return r.results[0]["out_dram"]
```

```python
from contextlib import ExitStack

import concourse.bass as bass
from concourse import mybir

F32 = mybir.dt.float32
F32R = mybir.dt.float32r
ALU = mybir.AluOpType
ACT = mybir.ActivationFunctionType

B, CH, T = 4, 32, 750
D = 128
H, HD = 4, 32
C = 125
NC = T // C
W4 = B * C
STK = 3 * CH + 2
ALPHA = 0.1
EPS_LN = 1e-5
EPS_L2 = 1e-12
NBUF = 3
assert NC * C == T and B * CH == 128 and H * HD == D


def build(nc, x, W_ve, b_ve, W_lin, b_lin, basis, wq, wk, v_coeffs, o_coeffs, logits, out_scale,
          W1, b1, W2, b2, out):
    with ExitStack() as ctx:
        def sb(name, shape, dt=F32):
            return ctx.enter_context(nc.sbuf_tensor(name, shape, dt))

        def sem(name):
            return ctx.enter_context(nc.semaphore(name))

        IC = sb("ident_and_centring", [D, 2, D])
        ident, centre = IC[:, 0, :], IC[:, 1, :]
        block_mask = sb("block_mask", [D, H, HD])
        lo_rows = sb("lo_rows", [STK, 1])
        ones_blk = sb("ones_blk", [D, 2, B])
        w_lin = sb("w_lin", [D, D])
        ve_raw = sb("ve_raw", [D, CH + 1])
        VE = sb("ve_stack", [D, STK])
        BL = sb("b_lin_stack", [D, STK])
        wqk = sb("wqk", [D, 2 * D])
        w_basis = sb("w_basis", [D, D])
        w_vc = sb("w_vc", [D, D])
        w_oc = sb("w_oc", [D, D])
        w_1 = sb("w_1", [D, D])
        w_2 = sb("w_2", [D, D])
        b1_col = sb("b1_col", [D, 1])
        b2_row = sb("b2_row", [C, D])
        osc = sb("osc", [D, 1])
        b_lin_col = sb("b_lin_col", [D, 1])
        lin_T = sb("lin_T", [D, 2 * D])
        proj_T = sb("proj_T", [D, 3, STK])
        proj_rep = sb("proj_rep", [D, 3, B, CH])
        basis_ct = sb("basis_ct", [D, STK])
        tr4 = sb("tr4", [D, 4, D])
        w2_T = sb("w2_T", [D, D])
        o_T = sb("o_T", [D, D])
        w_hi = sb("w_hi", [STK, 4 * D], F32R)
        w_stk = sb("w_stk", [STK, 4 * D], F32R)
        Q0, K0, V0, H0 = 0, D, 2 * D, 3 * D
        gram = sb("gram", [D, 3, B, CH])
        gram_lin = sb("gram_lin", [D, 3])
        gram_c = sb("gram_c", [C, 3])

        lg_row = sb("lg_row", [C, H])
        lg_col = sb("lg_col", [D, 1])
        dec_row = sb("dec_row", [C, 3, H])
        dec_col = sb("dec_col", [D, 3])
        before = sb("before", [C, C])
        first_one = sb("first_one", [D, C + 1])
        powers = sb("powers", [D, C + 1])
        key_pow = sb("key_pow", [C, D])
        qry_pow, chunk_pow = powers[:, C - 1::-1], powers[:, C:C + 1]
        table_in = sb("table_in", [D, 1])
        dmask = sb("dmask", [C, H, C])

        xt = sb("xt", [D, T])
        xd = sb("xd", [D, T])
        keep = sb("keep", [D, T])
        last10 = sb("last10", [D, 1])
        s_lr = sb("s_lr", [D, T])
        s_rl = sb("s_rl", [D, T])
        z = sb("z", [D, T])
        z_hi = sb("z_hi", [D, T], F32R)
        z_lo = sb("z_lo", [D, T], F32R)
        z_stk = sb("z_stk", [STK, NC, B, C], F32R)
        quad = sb("quad", [D, 3, T])
        ss = sb("ss", [C, 3, NC * B])
        rstd = sb("rstd", [C, NC * B])
        nrm = sb("nrm", [C, 3, NC * B])
        nrm2 = sb("nrm2", [C, 2, NC * B])
        rec = sb("rec", [C, 2, NC * B])
        sc_qk = sb("sc_qk", [C, 2, NC * B])
        sc_v = sb("sc_v", [C, NC * B])
        minus_half = sb("minus_half", [C, B])

        def bufs(name, shape):
            return [sb(f"{name}{n}", shape) for n in range(NBUF)]

        h_tok = bufs("h_tok", [C, B, D])
        k_dec = bufs("k_dec", [C, B, D])
        v_sc = bufs("v_sc", [C, B, D])
        qT = bufs("qT", [D, B, C])
        kT = [sb(f"kT{n}", [D, H, B, C]) for n in range(2)]
        q_dec = bufs("q_dec", [D, B, C])
        prob = [sb(f"prob{n}", [C, H, B, C]) for n in range(2)]
        rT = bufs("rT", [D, B, C])
        state = bufs("state", [D, B, D])
        state_m = bufs("state_m", [D, B, D])
        h2 = bufs("h2", [C, B, D])
        h2_b = bufs("h2_b", [C, B, D])
        bn6 = bufs("bn6", [C, B, 6])
        mv = bufs("mv", [C, B, 2])
        ve2 = bufs("ve2", [C, B])
        rstd2 = bufs("rstd2", [C, B])
        xn = bufs("xn", [C, B, D])
        xT = bufs("xT", [D, B, C])
        gT = bufs("gT", [D, B, C])
        y = bufs("y", [C, B, D])

        kv_ps = ctx.enter_context(nc.psum_tensor("kv_ps", [128, 1024], F32))
        hx_ps, qr_ps, kf_ps, f2_ps, s0_ps, s1_ps = (
            ctx.enter_context(nc.psum_tensor(n, [128, 512], F32))
            for n in ("hx_ps", "qr_ps", "kf_ps", "f2_ps", "s0_ps", "s1_ps"))
        st_ps, at_ps = kv_ps[:, 0:512], kv_ps[:, 512:1024]
        sc_ps = [s0_ps, s1_ps]
        gram3 = at_ps[:, 0:3 * STK].rearrange("p (a b) -> p a b", a=3)

        x_in, lin_in, ve_in, bl_in, qk_in, bas_in, vo_in, f_in, row_in, dec_in = (
            sem(n) for n in ("x_in", "lin_in", "ve_in", "bl_in", "qk_in", "bas_in", "vo_in", "f_in",
                             "row_in", "dec_in"))
        pool_c, dv_c = sem("pool_c"), sem("dv_c")
        ident_ok, centre_ok, bl0_ok, lo_ok, mask_ok, tril_ok, ones_ok = (
            sem(n) for n in ("ident_ok", "centre_ok", "bl0_ok", "lo_ok", "mask_ok", "tril_ok", "ones_ok"))
        b1_in, osc_in, dec_u = sem("b1_in"), sem("osc_in"), sem("dec_u")
        one_ok, before_ok, table_ok, keypow_ps = (sem(n) for n in ("one_ok", "before_ok", "table_ok", "keypow_ps"))
        exp_ok, dec_ok, pow_ok, dmask_ok, keypow_ok, half_ok = (
            sem(n) for n in ("exp_ok", "dec_ok", "pow_ok", "dmask_ok", "keypow_ok", "half_ok"))
        ve_ok = sem("ve_ok")
        linT_ps, linT_ok, hrep_ps, projT_ps, projT_ok, qkrep_ps, qkT_ps, qkT_ok = (
            sem(n) for n in ("linT_ps", "linT_ok", "hrep_ps", "projT_ps", "projT_ok", "qkrep_ps",
                             "qkT_ps", "qkT_ok"))
        bct_ps, bct_ok, tr4_ps, tr4_ok, w2T_ps, w2T_ok, vo_ps, oT_ok = (
            sem(n) for n in ("bct_ps", "bct_ok", "tr4_ps", "tr4_ok", "w2T_ps", "w2T_ok", "vo_ps", "oT_ok"))
        rep_ok, kz_ok, whi_h, whi_qk, whi_v = (sem(n) for n in ("rep_ok", "kz_ok", "whi_h", "whi_qk", "whi_v"))
        whi_ok, wstk_ok = sem("whi_ok"), sem("wstk_ok")
        gram_ps, gramc_ps, gram_ok, gramc_ok = (
            sem(n) for n in ("gram_ps", "gramc_ps", "gram_ok", "gramc_ok"))
        z_ok, zhi_ok, zlo_ok, zstk_v, zstk_d, zstk_a, zone_ok = (
            sem(n) for n in ("z_ok", "zhi_ok", "zlo_ok", "zstk_v", "zstk_d", "zstk_a", "zone_ok"))
        quad_ps, quad_ok, ss_ps, ss_ok, pw_ok, scale_ok, stat_v = (
            sem(n) for n in ("quad_ps", "quad_ok", "ss_ps", "ss_ok", "pw_ok", "scale_ok", "stat_v"))
        (qkT_s, qT_ok, kT_ok, kv_s, kd_ok, vs_ok, h_s, h_ok, score_s, prob_ok, qd_ok, rT_s, rT_ok, st_s, st_ok,
         stm_ok, at_s, h2_ok, bn_ok, mv_ok, ve2_ok, rstd2_ok, xn_ok, xT_s, xT_ok, f1_s, gT_ok, h2b_ok, f2_s,
         y_ok) = (
            sem(n) for n in ("qkT_s", "qT_ok", "kT_ok", "kv_s", "kd_ok", "vs_ok", "h_s", "h_ok", "score_s",
                             "prob_ok", "qd_ok", "rT_s", "rT_ok", "st_s", "st_ok", "stm_ok", "at_s", "h2_ok",
                             "bn_ok", "mv_ok", "ve2_ok", "rstd2_ok", "xn_ok", "xT_s", "xT_ok", "f1_s", "gT_ok",
                             "h2b_ok", "f2_s", "y_ok"))
        z_rest, zhi_rest, zlo_rest, zone_rest = (sem(n) for n in ("z_rest", "zhi_rest", "zlo_rest", "zone_rest"))
        out_ok = [sem(f"out_ok{n}") for n in range(NBUF)]

        GROUPS = [(NC - 1, NC), (0, NC - 1)]
        MID = 3 * C
        QUADS = [[(a, T - C, T, qr_ps, a * C) for a in range(3)],
                 [(0, 0, MID, kf_ps, 0), (1, 0, MID, f2_ps, 0), (2, 0, MID, s0_ps, 0),
                  (0, MID, T - C, s1_ps, 0), (1, MID, T - C, s1_ps, T - C - MID), (2, MID, T - C, kf_ps, 0)]]

        def span(whole, halves, part):
            return (whole, 0, B) if part is None else (halves[part], part * B // 2, (part + 1) * B // 2)

        def out_bank(i, b):
            return st_ps if i == NC - 1 and b >= B // 2 else at_ps

        def batches(part):
            return (0, B) if part is None else (part * B // 2, (part + 1) * B // 2)

        block = ctx.enter_context(nc.Block())

        @block.sync
        def _(sp):
            sp.dma_start(xt[:, :], x.rearrange("b c t -> (b c) t")).then_inc(x_in, 16)
            sp.dma_start(ve_raw[:, 0:CH], W_ve).then_inc(ve_in, 16)
            sp.dma_start(ve_raw[:, CH:CH + 1], b_ve.unsqueeze(1)).then_inc(ve_in, 16)
            sp.dma_start(wqk[:, 0:D], wq).then_inc(qk_in, 16)
            sp.dma_start(wqk[:, D:2 * D], wk).then_inc(qk_in, 16)
            sp.dma_start(w_basis[:, :], basis).then_inc(bas_in, 16)
            sp.dma_start(w_vc[:, :], v_coeffs).then_inc(vo_in, 16)
            sp.dma_start(w_oc[:, :], o_coeffs).then_inc(vo_in, 16)
            sp.dma_start(w_1[:, :], W1).then_inc(f_in, 16)
            sp.dma_start(w_2[:, :], W2).then_inc(f_in, 16)
            for part, src in ((0, z_hi), (2, z_hi), (1, z_lo)):
                sp.wait_ge(*((zhi_rest, 1), (zlo_rest, 1), (zhi_rest, 1))[part])
                for b in range(B):
                    sp.dma_start(z_stk[part * CH:(part + 1) * CH, 0:NC - 1, b, :].bitcast(F32),
                                 src[CH * b:CH * b + CH, 0:(NC - 1) * C].bitcast(F32)
                                 .rearrange("p (c t) -> p c t", t=C)).then_inc(zstk_d, 16)
            for i in range(NC - 1):
                c = NC - 1 - i
                sp.wait_ge(y_ok, i + 1)
                sp.dma_start(out[:, c * C:(c + 1) * C, :].rearrange("b t f -> t b f"),
                             y[i % NBUF][:, :, :]).then_inc(out_ok[i % NBUF], 16)
            for part, b0 in enumerate((0, B // 2)):
                sp.wait_ge(y_ok, NC + part)
                sp.dma_start(out[b0:b0 + B // 2, 0:C, :].rearrange("b t f -> t b f"),
                             y[(NC - 1) % NBUF][:, b0:b0 + B // 2, :]).then_inc(out_ok[(NC - 1) % NBUF], 16)
            for n in range(NBUF):
                sp.wait_ge(out_ok[n], 16 * (NC // NBUF + (n == (NC - 1) % NBUF)))

        @block.gpsimd
        def _(pool):
            pool.memset(ident, 0.0).then_inc(pool_c, 1)
            pool.memset(BL[:, :], 0.0).then_inc(bl0_ok, 1)
            pool.wait_ge(pool_c, 1)
            pool.affine_select(out=ident, in_=ident, compare_op=ALU.not_equal, fill=1.0, base=0,
                               pattern=[[-1, D]], channel_multiplier=1).then_inc(ident_ok, 1)
            pool.wait_ge(ident_ok, 1)
            pool.memset(z_stk[3 * CH:STK, NC - 1, :, :].bitcast(F32), 1.0).then_inc(zone_ok, 1)
            pool.dma_start(lg_row[:, :], logits.unsqueeze(0).broadcast_to([C, H])).then_inc(dec_in, 16)
            pool.dma_start(lg_col[:, :], logits.unsqueeze(1).unsqueeze(2).broadcast_to([H, HD, 1]))\
                .then_inc(dec_in, 16)
            pool.wait_ge(zone_ok, 1)
            pool.memset(kT[0][:, :, :, :], 0.0).then_inc(kz_ok, 1)
            pool.memset(before[:, :], 0.0).then_inc(pool_c, 1)
            pool.wait_ge(pool_c, 2)
            pool.affine_select(out=before[:, :], in_=before[:, :], compare_op=ALU.not_equal, fill=1.0, base=-1,
                               pattern=[[-1, C]], channel_multiplier=1).then_inc(before_ok, 1)
            pool.memset(block_mask[:, :, :], 1.0).then_inc(pool_c, 1)
            pool.wait_ge(pool_c, 3)
            pool.affine_select(out=block_mask[:, :, :], in_=block_mask[:, :, :], compare_op=ALU.is_ge, fill=0.0,
                               base=0, pattern=[[-HD, H], [0, HD]], channel_multiplier=1).then_inc(pool_c, 1)
            pool.wait_ge(pool_c, 4)
            pool.affine_select(out=block_mask[:, :, :], in_=block_mask[:, :, :], compare_op=ALU.is_ge, fill=0.0,
                               base=HD - 1, pattern=[[HD, H], [0, HD]], channel_multiplier=-1)\
                .then_inc(mask_ok, 1)
            pool.dma_start(osc[:, :], out_scale.unsqueeze(0).broadcast_to([D, 1])).then_inc(osc_in, 16)
            pool.dma_start(b1_col[:, :], b1.unsqueeze(1)).then_inc(b1_in, 16)
            pool.wait_ge(f_in, 32)
            for w in (w_1, w_2):
                pool.affine_select(out=w[:, :], in_=w[:, :], compare_op=ALU.is_ge, fill=0.0, base=0,
                                   pattern=[[-1, D]], channel_multiplier=1).then_inc(tril_ok, 1)
            pool.dma_start(b2_row[:, :], b2.unsqueeze(0).broadcast_to([C, D])).then_inc(row_in, 16)
            pool.wait_ge(mask_ok, 1)
            pool.tensor_copy(ones_blk[:, 1, :], block_mask[:, :, 0]).then_inc(ones_ok, 1)
            pool.tensor_scalar(ones_blk[:, 0, :], block_mask[:, :, 0], 1.0 / D, None, ALU.mult)\
                .then_inc(ones_ok, 1)
            pool.memset(minus_half[:, :], -0.5).then_inc(half_ok, 1)
            pool.wait_ge(dv_c, 6)
            pool.tensor_tensor(z[:, 0:T - C], s_lr[:, 0:T - C], s_rl[:, 0:T - C], ALU.add).then_inc(z_rest, 1)
            pool.wait_ge(ones_ok, 2)
            pool.wait_ge(half_ok, 1)
            pool.wait_ge(z_rest, 1)
            pool.memset(z_stk[3 * CH:STK, 0:NC - 1, :, :].bitcast(F32), 1.0).then_inc(zone_rest, 1)
            pool.wait_ge(zhi_rest, 1)
            pool.wait_ge(zone_rest, 1)
            pool.tensor_tensor(z_lo[:, 0:T - C], z[:, 0:T - C], z_hi[:, 0:T - C].bitcast(F32), ALU.subtract)\
                .then_inc(zlo_rest, 1)
            pool.memset(kT[1][:, :, :, :], 0.0).then_inc(kz_ok, 1)

            def distance(i):
                n = i % NBUF
                pool.wait_ge(qT_ok, i + 1)
                pool.wait_ge(pow_ok, 1)
                if i > NBUF:
                    pool.wait_ge(rT_s, i - NBUF + 1)
                pool.tensor_tensor(q_dec[n][:, :, :], qT[n][:, :, :],
                                   qry_pow.unsqueeze(1).broadcast_to([D, B, C]), ALU.mult).then_inc(qd_ok, 1)

            def mask_state(i):
                n = i % NBUF
                pool.wait_ge(st_ok, i + 1)
                if i >= NBUF:
                    pool.wait_ge(rT_s, i - NBUF + 2)
                pool.tensor_tensor(state_m[n][:, :, :], state[n][:, :, :],
                                   block_mask[:, :, :].rearrange("p h d -> p (h d)").unsqueeze(1)
                                   .broadcast_to([D, B, D]), ALU.mult).then_inc(stm_ok, 1)

            def rsqrt(i, part=None):
                n, (b0, b1) = i % NBUF, batches(part)
                pool.wait_ge(mv_ok, B * i + b1)
                pool.tensor_scalar(ve2[n][:, b0:b1], mv[n][:, b0:b1, 1], EPS_LN, None, ALU.add).then_inc(ve2_ok, 1)
                pool.wait_ge(ve2_ok, i + 1 + (part or 0))
                pool.tensor_tensor(rstd2[n][:, b0:b1], ve2[n][:, b0:b1], minus_half[:, b0:b1], ALU.pow)\
                    .then_inc(rstd2_ok, 1)

            def add_b2(i, part=None):
                n, (b0, b1) = i % NBUF, batches(part)
                pool.wait_ge(row_in, 16)
                if i >= NBUF:
                    pool.wait_ge(y_ok, i - NBUF + 1)
                pool.tensor_tensor(h2_b[n][:, b0:b1, :], h2[n][:, b0:b1, :],
                                   b2_row[:, :].unsqueeze(1).broadcast_to([C, b1 - b0, D]), ALU.add)\
                    .then_inc(h2b_ok, 1)

            for i in range(NC - 1):
                mask_state(i)
                distance(i + 1)
                rsqrt(i)
                add_b2(i)
            for part in range(2):
                rsqrt(NC - 1, part)
            for part in range(2):
                add_b2(NC - 1, part)

        @block.scalar
        def _(act):
            act.dma_start(w_lin[:, :], W_lin).then_inc(lin_in, 16)
            act.dma_start(b_lin_col[:, 0:1], b_lin.unsqueeze(1)).then_inc(bl_in, 16)
            act.wait_ge(dv_c, 1)
            act.activation(table_in[:, :], xd[:, 0:1], ACT.Exp).then_inc(table_ok, 1)
            act.wait_ge(linT_ps, 1)
            act.activation(lin_T[:, :], kv_ps[:, 0:2 * D], ACT.Copy).then_inc(linT_ok, 1)
            act.wait_ge(projT_ps, 1)
            act.activation(proj_T[:, 0, :], hx_ps[:, 0:STK], ACT.Copy).then_inc(projT_ok, 1)
            act.wait_ge(hrep_ps, 1)
            act.activation(w_hi[:, H0:H0 + D], s1_ps[0:STK, 0:D], ACT.Copy).then_inc(whi_h, 1)
            act.wait_ge(zhi_ok, 1)
            for b in range(B):
                act.activation(z_stk[2 * CH:3 * CH, NC - 1, b, :],
                               z_hi[CH * b:CH * b + CH, (NC - 1) * C:T].bitcast(F32), ACT.Copy)\
                    .then_inc(zstk_a, 1)
            act.wait_ge(qkrep_ps, 1)
            act.activation(w_hi[:, Q0:V0], qr_ps[0:STK, 0:2 * D], ACT.Copy).then_inc(whi_qk, 1)

            def q_out(i):
                act.wait_ge(qkT_s, 2 * i + 1)
                if i >= NBUF:
                    act.wait_ge(qd_ok, i - NBUF)
                    act.wait_ge(score_s, H * (i - NBUF + 1))
                act.activation(qT[i % NBUF][:, :, :].rearrange("p b t -> p (b t)"), qr_ps[:, 0:W4], ACT.Copy)\
                    .then_inc(qT_ok, 1)

            def k_out(i, heads=range(H)):
                act.wait_ge(qkT_s, 2 * i + 2)
                if i < 2:
                    act.wait_ge(kz_ok, i + 1)
                else:
                    act.wait_ge(score_s, H * (i - 1))
                for h in heads:
                    rows = slice(h * HD, (h + 1) * HD)
                    act.activation(kT[i % 2][rows, h, :, :].rearrange("p b t -> p (b t)"), kf_ps[rows, 0:W4],
                                   ACT.Copy).then_inc(kT_ok, 1)

            def h_out(i):
                act.wait_ge(h_s, i + 1)
                if i >= NBUF:
                    act.wait_ge(h2_ok, B * (i - NBUF + 1))
                act.activation(h_tok[i % NBUF][:, :, :].rearrange("p b f -> p (b f)"), hx_ps[0:C, :], ACT.Copy)\
                    .then_inc(h_ok, 1)

            def r_out(i):
                act.wait_ge(rT_s, i + 1)
                if i >= NBUF:
                    act.wait_ge(at_s, i - NBUF + 1)
                act.activation(rT[i % NBUF][:, :, :].rearrange("p b t -> p (b t)"), qr_ps[:, 0:W4], ACT.Copy)\
                    .then_inc(rT_ok, 1)

            def ffn_in(i, part=None):
                n, (ps, b0, b1) = i % NBUF, span(hx_ps, (kf_ps, s0_ps), part)
                act.wait_ge(xT_s, i + 1 + (part or 0))
                if i >= NBUF:
                    act.wait_ge(f1_s, i - NBUF + 1)
                act.activation(xT[n][:, b0:b1, :].rearrange("p b t -> p (b t)"), ps[:, b0 * C:b1 * C], ACT.Copy)\
                    .then_inc(xT_ok, 1)

            def ffn_gelu(i, part=None):
                n, (ps, b0, b1) = i % NBUF, span(f2_ps, (f2_ps, s1_ps), part)
                act.wait_ge(f1_s, i + 1 + (part or 0))
                if i == 0:
                    act.wait_ge(b1_in, 16)
                if i >= NBUF:
                    act.wait_ge(f2_s, i - NBUF + 1)
                act.activation(gT[n][:, b0:b1, :].rearrange("p b t -> p (b t)"), ps[:, b0 * C:b1 * C], ACT.Gelu,
                               bias=b1_col[:, 0:1]).then_inc(gT_ok, 1)

            def roots(group):
                c0, c1 = GROUPS[group]
                act.wait_ge(ss_ok, 3 * (group + 1))
                act.activation(nrm[:, :, c0 * B:c1 * B], ss[:, :, c0 * B:c1 * B], ACT.Sqrt).then_inc(pw_ok, 1)

            act.wait_ge(bct_ps, 1)
            act.activation(basis_ct[:, :], f2_ps[:, 0:STK], ACT.Copy).then_inc(bct_ok, 1)
            act.wait_ge(dec_in, 32)
            act.activation(dec_row[:, 0, :], lg_row[:, :], ACT.Exp, scale=-1.0).then_inc(exp_ok, 1)
            act.activation(dec_col[:, 0:1], lg_col[:, :], ACT.Exp, scale=-1.0).then_inc(exp_ok, 1)
            q_out(0)
            k_out(0, range(0, H // 2))
            act.wait_ge(tr4_ps, 1)
            act.activation(tr4[:, :, :].rearrange("p a b -> p (a b)"), st_ps, ACT.Copy)\
                .then_inc(tr4_ok, 1)
            act.wait_ge(z_rest, 1)
            act.activation(z_hi[:, 0:T - C], z[:, 0:T - C], ACT.Copy).then_inc(zhi_rest, 1)
            act.wait_ge(vo_ps, 1)
            act.activation(w_hi[:, V0:H0], f2_ps[0:STK, 0:D], ACT.Copy).then_inc(whi_v, 1)
            h_out(0)
            act.wait_ge(vo_ps, 2)
            act.wait_ge(w2T_ps, 1)
            act.wait_ge(osc_in, 16)
            act.activation(o_T[:, :], kv_ps[:, 0:D], ACT.Copy, scale=osc[:, 0:1]).then_inc(oT_ok, 1)
            act.activation(w2_T[:, :], kv_ps[:, D:2 * D], ACT.Copy).then_inc(w2T_ok, 1)
            k_out(0, range(H // 2, H))
            roots(0)
            r_out(0)
            q_out(1)
            k_out(1)
            roots(1)
            h_out(1)
            act.activation(table_in[:, :], xd[:, 0:1], ACT.Gelu).then_inc(table_ok, 1)
            for i in range(1, NC):
                r_out(i)
                if i < NC - 1:
                    q_out(i + 1)
                ffn_in(i - 1)
                if i < NC - 1:
                    k_out(i + 1, [0, 1])
                ffn_gelu(i - 1)
                if i < NC - 1:
                    k_out(i + 1, [2, 3])
                    h_out(i + 1)
            for part in range(2):
                ffn_in(NC - 1, part)
            for part in range(2):
                ffn_gelu(NC - 1, part)

        @block.vector
        def _(dve):
            dve.memset(xd[:, 0:1], 0.0).then_inc(dv_c, 1)
            dve.memset(lo_rows[:, :], 0.0).then_inc(lo_ok, 1)
            dve.wait_ge(lo_ok, 1)
            dve.memset(lo_rows[2 * CH:3 * CH, :], -1.0).then_inc(lo_ok, 1)
            dve.memset(keep[:, :], 1.0 - ALPHA).then_inc(dv_c, 1)
            dve.memset(first_one[:, 1:C + 1], 0.0).then_inc(one_ok, 1)
            dve.memset(first_one[:, 0:1], 1.0).then_inc(one_ok, 1)
            dve.wait_ge(ident_ok, 1)
            dve.tensor_scalar(centre, ident, -1.0 / D, None, ALU.add).then_inc(centre_ok, 1)
            dve.tensor_scalar(lo_rows[3 * CH:STK, :], ident[3 * CH:STK, STK - 1:STK], -1.0, None, ALU.mult)\
                .then_inc(lo_ok, 1)
            dve.wait_ge(x_in, 16)
            dve.tensor_tensor(xd[:, 1:T], xt[:, 1:T], xt[:, 0:T - 1], ALU.subtract).then_inc(dv_c, 1)
            dve.wait_ge(ve_in, 32)
            dve.tensor_scalar(VE[:, 0:3 * CH].rearrange("p (a c) -> p a c", a=3),
                              ve_raw[:, 0:CH].unsqueeze(1).broadcast_to([D, 3, CH]), 0.5 * ALPHA, None,
                              ALU.mult).then_inc(ve_ok, 1)
            dve.tensor_copy(VE[:, 3 * CH:STK], ve_raw[:, CH:CH + 1].broadcast_to([D, 2])).then_inc(ve_ok, 1)
            dve.wait_ge(bl_in, 16)
            dve.wait_ge(bl0_ok, 1)
            dve.tensor_copy(BL[:, 3 * CH:STK], b_lin_col[:, 0:1].broadcast_to([D, 2])).then_inc(bl0_ok, 1)
            dve.wait_ge(dv_c, 3)
            dve.tensor_scalar(last10[:, :], xd[:, T - 1:T], 1.0 / ALPHA, None, ALU.mult).then_inc(dv_c, 1)
            dve.tensor_tensor_scan(s_lr[:, :], keep[:, :], xd[:, :], 0.0, ALU.mult, ALU.add).then_inc(dv_c, 1)
            dve.wait_ge(dv_c, 4)
            dve.tensor_tensor_scan(s_rl[:, ::-1], keep[:, :], xd[:, ::-1], last10[:, 0:1], ALU.mult,
                                   ALU.add).then_inc(dv_c, 1)
            dve.wait_ge(dv_c, 6)

            dve.tensor_tensor(z[:, T - C:T], s_lr[:, T - C:T], s_rl[:, T - C:T], ALU.add).then_inc(z_ok, 1)
            dve.wait_ge(z_ok, 1)
            dve.tensor_copy(z_hi[:, T - C:T], z[:, T - C:T]).then_inc(zhi_ok, 1)
            dve.wait_ge(zhi_ok, 1)
            dve.tensor_tensor(z_lo[:, T - C:T], z[:, T - C:T], z_hi[:, T - C:T].bitcast(F32), ALU.subtract)\
                .then_inc(zlo_ok, 1)
            for part, src in ((0, z_hi), (1, z_lo)):
                dve.wait_ge((zhi_ok, zlo_ok)[part], 1)
                for b in range(B):
                    dve.tensor_copy(z_stk[part * CH:(part + 1) * CH, NC - 1, b, :],
                                    src[CH * b:CH * b + CH, (NC - 1) * C:T].bitcast(F32)).then_inc(zstk_v, 1)

            def stack_w(ps, c0, c1, hi_ok):
                dve.wait_ge(hi_ok, 1)
                dve.scalar_tensor_tensor(out=w_stk[:, c0:c1], in0=w_hi[:, c0:c1].bitcast(F32),
                                         scalar=lo_rows[:, 0:1], in1=ps, op0=ALU.mult, op1=ALU.add)\
                    .then_inc(wstk_ok, 1)
            dve.wait_ge(lo_ok, 3)
            stack_w(qr_ps[0:STK, 0:2 * D], Q0, V0, whi_qk)
            stack_w(s1_ps[0:STK, 0:D], H0, H0 + D, whi_h)
            dve.wait_ge(qkT_ps, 1)
            dve.tensor_copy(proj_T[:, 1:3, :].rearrange("p a b -> p (a b)"), at_ps[:, 0:2 * STK])\
                .then_inc(qkT_ok, 1)
            dve.wait_ge(qkT_ok, 1)
            dve.wait_ge(projT_ok, 1)
            dve.tensor_copy(proj_rep[:, :, :, :], proj_T[:, :, 0:CH].unsqueeze(2).broadcast_to([D, 3, B, CH]))\
                .then_inc(rep_ok, 1)
            dve.wait_ge(exp_ok, 2)
            dve.tensor_scalar(dec_row[:, 1, :], dec_row[:, 0, :], 1.0, None, ALU.add).then_inc(dec_u, 1)
            dve.tensor_scalar(dec_col[:, 1:2], dec_col[:, 0:1], 1.0, None, ALU.add).then_inc(dec_u, 1)
            dve.wait_ge(dec_u, 2)
            dve.reciprocal(dec_row[:, 2, :], dec_row[:, 1, :]).then_inc(dec_ok, 1)
            dve.reciprocal(dec_col[:, 2:3], dec_col[:, 1:2]).then_inc(dec_ok, 1)
            dve.wait_ge(dec_ok, 2)
            dve.wait_ge(before_ok, 1)
            dve.wait_ge(one_ok, 2)
            for h in range(H):
                ins = dve.tensor_tensor_scan(dmask[:, h, ::-1], dec_row[:, 2, h:h + 1].broadcast_to([C, C]),
                                             before[:, ::-1], 0.0, ALU.mult, ALU.add)
            ins.then_inc(dmask_ok, 1)
            dve.tensor_tensor_scan(powers[:, :], dec_col[:, 2:3].broadcast_to([D, C + 1]), first_one[:, :],
                                   0.0, ALU.mult, ALU.add).then_inc(pow_ok, 1)
            dve.wait_ge(gram_ps, 1)
            dve.wait_ge(mask_ok, 1)
            for a in range(3):
                dve.tensor_tensor(gram[:, a, :, :], gram3[:, a, 0:CH].unsqueeze(1).broadcast_to([D, B, CH]),
                                  block_mask[:, :, :], ALU.mult).then_inc(gram_ok, 1)
            dve.tensor_scalar(gram_lin[:, :], gram3[:, :, 3 * CH], 2.0, None, ALU.mult).then_inc(gram_ok, 1)
            dve.tensor_scalar(gram_c[:, 0:1], at_ps[0:C, 3 * STK:3 * STK + 1], 1.0 / D, EPS_LN, ALU.mult, ALU.add)\
                .then_inc(gram_ok, 1)
            dve.tensor_copy(gram_c[:, 1:3], at_ps[0:C, 3 * STK + 1:3 * STK + 3]).then_inc(gram_ok, 1)
            stack_w(f2_ps[0:STK, 0:D], V0, H0, whi_v)

            def quads(group):
                for k, (a, t0, t1, bank, col) in enumerate(QUADS[group]):
                    dve.wait_ge(quad_ps, 3 if group == 0 else (4, 5, 6, 8, 8, 9)[k])
                    dve.scalar_tensor_tensor(out=quad[:, a, t0:t1], in0=bank[:, col:col + t1 - t0],
                                             scalar=gram_lin[:, a:a + 1], in1=z[:, t0:t1], op0=ALU.add,
                                             op1=ALU.mult).then_inc(quad_ok, 1)

            def sums(group):
                c0, c1 = GROUPS[group]
                dve.wait_ge(ss_ps, group + 1)
                for a in range(3):
                    dve.tensor_scalar(ss[:, a, c0 * B:c1 * B], (hx_ps, f2_ps)[group][0:C, (a * NC + c0) * B:(a * NC + c1) * B],
                                      gram_c[:, a:a + 1], EPS_LN if a == 0 else 0.0, ALU.add, ALU.max)\
                        .then_inc(ss_ok, 1)

            def scales(group):
                k, cols = 5 * group, slice(GROUPS[group][0] * B, GROUPS[group][1] * B)
                dve.wait_ge(pw_ok, group + 1)
                dve.reciprocal(rstd[:, cols], nrm[:, 0, cols]).then_inc(stat_v, 1)
                dve.wait_ge(stat_v, k + 1)
                rb = rstd[:, cols].unsqueeze(1).broadcast_to([C, 2, cols.stop - cols.start])
                dve.tensor_tensor(nrm2[:, :, cols], nrm[:, 1:3, cols], rb, ALU.mult).then_inc(stat_v, 1)
                dve.wait_ge(stat_v, k + 2)
                dve.tensor_scalar(nrm2[:, :, cols], nrm2[:, :, cols], EPS_L2, None, ALU.max).then_inc(stat_v, 1)
                dve.wait_ge(stat_v, k + 3)
                dve.reciprocal(rec[:, :, cols], nrm2[:, :, cols]).then_inc(stat_v, 1)
                dve.wait_ge(stat_v, k + 4)
                dve.tensor_tensor(sc_qk[:, :, cols], rec[:, :, cols], rb, ALU.mult).then_inc(stat_v, 1)
                dve.wait_ge(stat_v, k + 5)
                dve.tensor_tensor(sc_v[:, cols], sc_qk[:, 1, cols], rstd[:, cols], ALU.mult).then_inc(scale_ok, 1)

            kv = kv_ps[0:C, :].rearrange("p (b f) -> p b f", b=B)

            def probs(i, h):
                if h == 0 and i == 0:
                    dve.wait_ge(dmask_ok, 1)
                if h == 0 and i >= 2:
                    dve.wait_ge(rT_s, i - 1)
                dve.wait_ge(score_s, H * i + h + 1)
                dve.tensor_tensor(prob[i % 2][:, h, :, :],
                                  sc_ps[h % 2][0:C, 0:W4].rearrange("p (b t) -> p b t", b=B),
                                  dmask[:, h, :].unsqueeze(1).broadcast_to([C, B, C]), ALU.mult)\
                    .then_inc(prob_ok, 1)

            def keys(i):
                n = i % NBUF
                dve.wait_ge(kv_s, 2 * i + 2)
                if i == 0:
                    dve.wait_ge(keypow_ok, 1)
                if i >= NBUF:
                    dve.wait_ge(st_s, i - NBUF + 1)
                dve.tensor_tensor(k_dec[n][:, :, :], kv[:, :, 0:D],
                                  key_pow[:, :].unsqueeze(1).broadcast_to([C, B, D]), ALU.mult).then_inc(kd_ok, 1)

            def values(i):
                n, c = i % NBUF, NC - 1 - i
                dve.wait_ge(kv_s, 2 * i + 2)
                dve.wait_ge(scale_ok, 1 if i == 0 else 2)
                if i >= NBUF:
                    dve.wait_ge(rT_s, i - NBUF + 1)
                dve.tensor_tensor(v_sc[n][:, :, :], kv[:, :, D:2 * D],
                                  sc_v[:, c * B:c * B + B].unsqueeze(2)
                                  .broadcast_to([C, B, D]), ALU.mult).then_inc(vs_ok, 1)

            def carry_on(i):
                dve.wait_ge(st_s, i + 1)
                new = state[i % NBUF][:, :, :].rearrange("p b f -> p (b f)")
                if i >= NBUF:
                    dve.wait_ge(stm_ok, i - NBUF + 1)
                if i == 0:
                    dve.tensor_copy(new, st_ps).then_inc(st_ok, 1)
                else:
                    dve.wait_ge(st_ok, i)
                    dve.wait_ge(pow_ok, 1)
                    dve.scalar_tensor_tensor(
                        out=new, in0=state[(i - 1) % NBUF][:, :, :].rearrange("p b f -> p (b f)"),
                        scalar=chunk_pow, in1=st_ps, op0=ALU.mult, op1=ALU.add).then_inc(st_ok, 1)

            def last_sum(i, part=None):
                n, (ps, b0, b1) = i % NBUF, span(hx_ps, (kf_ps, qr_ps), part)
                dve.wait_ge(f2_s, i + 1 + (part or 0))
                dve.wait_ge(h2b_ok, i + 1 + (part or 0))
                if i >= NBUF:
                    dve.wait_ge(out_ok[n], 16 * (i // NBUF))
                dve.tensor_tensor(y[n][:, b0:b1, :], ps[0:C, b0 * D:b1 * D].rearrange("p (b f) -> p b f", f=D),
                                  h2_b[n][:, b0:b1, :], ALU.add).then_inc(y_ok, 1)

            def residual(i, part=None):
                n, c, (b0, b1) = i % NBUF, NC - 1 - i, batches(part)
                dve.wait_ge(at_s, i + 1 + (part or 0))
                dve.wait_ge(h_ok, i + 1)
                if i >= NBUF:
                    dve.wait_ge(h2b_ok, i - NBUF + 1)
                for b in range(b0, b1):
                    at = c * B + b
                    dve.scalar_tensor_tensor(out=h2[n][:, b, :], in0=out_bank(i, b)[0:C, b * D:(b + 1) * D],
                                             scalar=sc_qk[:, 0, at:at + 1],
                                             in1=h_tok[n][:, b, :], op0=ALU.mult, op1=ALU.add)\
                        .then_inc(h2_ok, 1)

            def statistics(i, part=None):
                n, (b0, b1) = i % NBUF, batches(part)
                for b in range(b0, b1):
                    dve.wait_ge(h2_ok, B * i + b + 1)
                    dve.bn_stats(bn6[n][:, b, :], h2[n][:, b, :]).then_inc(bn_ok, 1)
                for b in range(b0, b1):
                    dve.wait_ge(bn_ok, B * i + b + 1)
                    dve.bn_aggr(mv[n][:, b, :], bn6[n][:, b, :]).then_inc(mv_ok, 1)

            def normed(i, part=None):
                n, (b0, b1) = i % NBUF, batches(part)
                dve.wait_ge(rstd2_ok, i + 1 + (part or 0))
                if i >= NBUF:
                    dve.wait_ge(xT_s, i - NBUF + 1)
                for b in range(b0, b1):
                    dve.tensor_scalar(xn[n][:, b, :], h2[n][:, b, :], mv[n][:, b, 0:1], rstd2[n][:, b:b + 1],
                                      ALU.subtract, ALU.mult).then_inc(xn_ok, 1)

            probs(0, 0)
            probs(0, 1)
            dve.wait_ge(keypow_ps, 1)
            dve.tensor_copy(key_pow[:, :], f2_ps[0:C, 0:D]).then_inc(keypow_ok, 1)
            quads(0)
            probs(0, 2)
            sums(0)
            probs(0, 3)
            scales(0)
            values(0)
            keys(0)
            quads(1)
            carry_on(0)
            residual(0)
            for i in range(1, NC):
                probs(i, 0)
                statistics(i - 1)
                if i == 1:
                    sums(1)
                else:
                    last_sum(i - 2)
                probs(i, 1)
                if i == 1:
                    scales(1)
                probs(i, 2)
                values(i)
                probs(i, 3)
                if i < NC - 1:
                    keys(i)
                normed(i - 1)
                if i < NC - 1:
                    carry_on(i)
                    residual(i)
            for part in range(2):
                residual(NC - 1, part)
                statistics(NC - 1, part)
            for part in range(2):
                normed(NC - 1, part)
            last_sum(NC - 2)
            for part in range(2):
                last_sum(NC - 1, part)

        @block.tensor
        def _(pe):
            pe.wait_ge(lin_in, 16)
            pe.wait_ge(centre_ok, 1)
            pe.matmul(kv_ps[:, 0:2 * D], w_lin[:, :], IC[:, :, :].rearrange("p a b -> p (a b)"),
                      start=True, stop=True).then_inc(linT_ps, 1)
            pe.wait_ge(linT_ok, 1)
            pe.wait_ge(ve_ok, 2)
            pe.wait_ge(bl0_ok, 2)
            pe.matmul(hx_ps[:, 0:STK], lin_T[:, D:2 * D], VE[:, :], start=True, stop=False)
            pe.matmul(hx_ps[:, 0:STK], centre, BL[:, :], start=False, stop=True).then_inc(projT_ps, 1)
            pe.matmul(s1_ps[0:STK, 0:D], VE[:, :], lin_T[:, 0:D], start=True, stop=False)
            pe.matmul(s1_ps[0:STK, 0:D], BL[:, :], ident, start=False, stop=True).then_inc(hrep_ps, 1)
            pe.wait_ge(projT_ok, 1)
            pe.wait_ge(qk_in, 32)
            pe.matmul(qr_ps[0:STK, 0:2 * D], proj_T[:, 0, :], wqk[:, :], start=True, stop=True)\
                .then_inc(qkrep_ps, 1)
            pe.wait_ge(bas_in, 16)
            pe.matmul(f2_ps[:, 0:STK], w_basis[:, :], proj_T[:, 0, :], start=True, stop=True)\
                .then_inc(bct_ps, 1)
            pe.matmul(at_ps[:, 0:STK], wqk[:, 0:D], proj_T[:, 0, :], start=True, stop=True)
            pe.matmul(at_ps[:, STK:2 * STK], wqk[:, D:2 * D], proj_T[:, 0, :], start=True, stop=True)\
                .then_inc(qkT_ps, 1)

            def forms():
                pe.wait_ge(rep_ok, 1)
                for a in range(3):
                    pe.matmul(at_ps[:, a * STK:(a + 1) * STK], proj_rep[:, a, :, :].rearrange("p b c -> p (b c)"),
                              proj_T[:, a, :], start=True, stop=True)
                for a in range(3):
                    ins = pe.matmul(at_ps[0:C, 3 * STK + a:3 * STK + a + 1],
                                    proj_T[:, a, 3 * CH:3 * CH + 1].broadcast_to([D, C]),
                                    proj_T[:, a, 3 * CH:3 * CH + 1], start=True, stop=True)
                ins.then_inc(gram_ps, 1)

            def quads(group, pieces=(0, 1, 2)):
                if group == 0:
                    pe.wait_ge(gram_ok, 6)
                    pe.wait_ge(qT_ok, 1)
                for k in pieces:
                    a, t0, t1, bank, col = QUADS[group][k]
                    if group == 1:
                        for other, value in (((kT_ok, H),), ((keypow_ok, 1),), ((prob_ok, 3),), ((prob_ok, 4),), (),
                                             ((quad_ok, 4),))[k]:
                            pe.wait_ge(other, value)
                    pe.matmul(bank[:, col:col + t1 - t0], gram[:, a, :, :].rearrange("p b c -> p (b c)"),
                              z[:, t0:t1], start=True, stop=True).then_inc(quad_ps, 1)

            def sums(group, forms=range(3)):
                if group == 0:
                    pe.wait_ge(ones_ok, 2)
                    pe.wait_ge(h_ok, 1)
                pe.wait_ge(quad_ok, (3, 9)[group])
                for a in forms:
                    for c in range(*GROUPS[group]):
                        at = (a * NC + c) * B
                        ins = pe.matmul((hx_ps, f2_ps)[group][0:C, at:at + B], quad[:, a, c * C:(c + 1) * C],
                                        ones_blk[:, min(a, 1), :], start=True, stop=True)
                if 2 in forms:
                    ins.then_inc(ss_ps, 1)

            def project_q(i):
                if i > 0:
                    pe.wait_ge(rT_ok, i)
                pe.matmul(qr_ps[:, 0:W4], w_stk[:, Q0:Q0 + D],
                          z_stk[:, NC - 1 - i, :, :].rearrange("p b t -> p (b t)"),
                          start=True, stop=True).then_inc(qkT_s, 1)

            def project_k(i):
                if i == 1:
                    pe.wait_ge(quad_ok, 9)
                if i > 1:
                    pe.wait_ge(kT_ok, H * i)
                pe.matmul(kf_ps[:, 0:W4], w_stk[:, K0:K0 + D],
                          z_stk[:, NC - 1 - i, :, :].rearrange("p b t -> p (b t)"),
                          start=True, stop=True).then_inc(qkT_s, 1)

            def project_kv(i):
                c = NC - 1 - i
                if i == 0:
                    pe.wait_ge(oT_ok, 1)
                    pe.wait_ge(w2T_ok, 1)
                    pe.wait_ge(wstk_ok, 3)
                else:
                    pe.wait_ge(st_ok, i)
                for b in range(B):
                    if b == 2 and i == 0:
                        pe.wait_ge(gram_ok, 6)
                    if b == 2 and i > 0:
                        pe.wait_ge(h2_ok, B * i)
                    ins = pe.matmul(kv_ps[0:C, b * 2 * D:(b + 1) * 2 * D], z_stk[:, c, b, :],
                                    w_stk[:, K0:K0 + 2 * D], start=True, stop=True)
                    if b % 2:
                        ins.then_inc(kv_s, 1)

            def project_h(i):
                c = NC - 1 - i
                if i == 1:
                    pe.wait_ge(ss_ok, 3)
                if i > 1:
                    pe.wait_ge(y_ok, i - 1)
                for b in range(B):
                    ins = pe.matmul(hx_ps[0:C, b * D:(b + 1) * D], z_stk[:, c, b, :],
                                    w_stk[:, H0:H0 + D], start=True, stop=True)
                ins.then_inc(h_s, 1)

            def score(i, h):
                if h == 0:
                    pe.wait_ge(qT_ok, i + 1)
                pe.wait_ge(kT_ok, H * i + h + 1)
                if H * i + h >= 2:
                    pe.wait_ge(prob_ok, H * i + h - 1)
                for b in range(B):
                    ins = pe.matmul(sc_ps[h % 2][0:C, b * C:(b + 1) * C], kT[i % 2][:, h, b, :],
                                    qT[i % NBUF][:, b, :], start=True, stop=True)
                ins.then_inc(score_s, 1)

            def recall(i):
                pe.wait_ge(qd_ok, i)
                pe.wait_ge(stm_ok, i)
                for b in range(B):
                    pe.matmul(qr_ps[:, b * C:(b + 1) * C], state_m[(i - 1) % NBUF][:, b, :],
                              q_dec[i % NBUF][:, b, :], start=(b == 0), stop=False, skip_group_check=True)

            def retrieve(i):
                n = i % NBUF
                pe.wait_ge(vs_ok, i + 1)
                for b in range(B):
                    if b == 0:
                        pe.wait_ge(prob_ok, H * (i + 1))
                    for h in range(H):
                        cols = slice(h * HD, (h + 1) * HD)
                        ins = pe.matmul(qr_ps[cols, b * C:(b + 1) * C], v_sc[n][:, b, cols],
                                        prob[i % 2][:, h, b, :], start=(i == 0 and b == 0),
                                        stop=(b == B - 1), skip_group_check=True)
                ins.then_inc(rT_s, 1)

            def carry(i):
                n = i % NBUF
                pe.wait_ge(kd_ok, i + 1)
                pe.wait_ge(vs_ok, i + 1)
                for b in range(B):
                    ins = pe.matmul(st_ps[:, b * D:(b + 1) * D], k_dec[n][:, b, :], v_sc[n][:, b, :],
                                    start=True, stop=True)
                ins.then_inc(st_s, 1)

            def attention_out(i):
                n = i % NBUF
                pe.wait_ge(rT_ok, i + 1)
                for b in range(B):
                    ps = out_bank(i, b)
                    ins = pe.matmul(ps[0:C, b * D:(b + 1) * D], rT[n][:, b, :], o_T[:, :],
                                    start=True, stop=True)
                    if b == B - 1 or (i == NC - 1 and b == B // 2 - 1):
                        ins.then_inc(at_s, 1)

            def ffn_turn(i, part=None):
                n, (ps, b0, b1) = i % NBUF, span(hx_ps, (kf_ps, s0_ps), part)
                if part is None:
                    pe.wait_ge(h_ok, i + 2)
                for b in range(b0, b1):
                    pe.wait_ge(xn_ok, B * i + b + 1)
                    ins = pe.transpose(ps[:, b * C:(b + 1) * C], xn[n][:, b, :], ident[0:C, 0:C])
                ins.then_inc(xT_s, 1)

            def ffn_1(i, part=None):
                n, (ps, b0, b1) = i % NBUF, span(f2_ps, (f2_ps, s1_ps), part)
                pe.wait_ge(xT_ok, i + 1 + (part or 0))
                if i == 0:
                    pe.wait_ge(ss_ok, 6)
                pe.matmul(ps[:, b0 * C:b1 * C], tr4[:, 3, :], xT[n][:, b0:b1, :].rearrange("p b t -> p (b t)"),
                          start=True, stop=True).then_inc(f1_s, 1)

            def ffn_2(i, part=None):
                n, (ps, b0, b1) = i % NBUF, span(hx_ps, (kf_ps, qr_ps), part)
                pe.wait_ge(gT_ok, i + 1 + (part or 0))
                for b in range(b0, b1):
                    ins = pe.matmul(ps[0:C, b * D:(b + 1) * D], gT[n][:, b, :], w2_T[:, :],
                                    start=True, stop=True)
                ins.then_inc(f2_s, 1)

            pe.wait_ge(wstk_ok, 1)
            pe.wait_ge(zone_ok, 1)
            pe.wait_ge(zstk_v, 2 * B)
            pe.wait_ge(zstk_a, B)
            project_q(0)
            project_k(0)
            pe.wait_ge(wstk_ok, 2)
            project_h(0)
            pe.wait_ge(vo_in, 32)
            pe.wait_ge(tril_ok, 2)
            for j, w in enumerate((w_vc, w_oc, w_basis, w_1)):
                ins = pe.transpose(st_ps[:, j * D:(j + 1) * D], w[:, :], ident)
            ins.then_inc(tr4_ps, 1)
            forms()
            pe.wait_ge(tr4_ok, 1)
            pe.wait_ge(bct_ok, 1)
            pe.matmul(f2_ps[0:STK, 0:D], basis_ct[:, :], tr4[:, 0, :], start=True, stop=True)\
                .then_inc(vo_ps, 1)
            pe.matmul(kv_ps[:, 0:D], tr4[:, 1, :], tr4[:, 2, :], start=True, stop=True).then_inc(vo_ps, 1)
            pe.transpose(kv_ps[:, D:2 * D], w_2[:, :], ident).then_inc(w2T_ps, 1)
            score(0, 0)
            score(0, 1)
            pe.wait_ge(pow_ok, 1)
            pe.wait_ge(wstk_ok, 3)
            pe.transpose(f2_ps[0:C, 0:D], powers[:, 0:C], ident).then_inc(keypow_ps, 1)
            project_kv(0)
            quads(0)
            score(0, 2)
            sums(0)
            score(0, 3)
            quads(1, range(5))
            retrieve(0)
            quads(1, [5])
            carry(0)
            pe.wait_ge(zone_rest, 1)
            pe.wait_ge(zstk_d, 16 * 3 * B)
            project_q(1)
            project_k(1)
            attention_out(0)
            sums(1, [0])
            score(1, 0)
            for i in range(1, NC):
                if i == 1:
                    sums(1, [1])
                score(i, 1)
                if i == 1:
                    sums(1, [2])
                project_kv(i)
                score(i, 2)
                project_h(i)
                score(i, 3)
                recall(i)
                retrieve(i)
                if i < NC - 1:
                    carry(i)
                    project_q(i + 1)
                    project_k(i + 1)
                ffn_turn(i - 1)
                attention_out(i)
                ffn_1(i - 1)
                if i < NC - 1:
                    score(i + 1, 0)
                ffn_2(i - 1)
            for part in range(2):
                ffn_turn(NC - 1, part)
            for part in range(2):
                ffn_1(NC - 1, part)
            for part in range(2):
                ffn_2(NC - 1, part)


_INS = ['x', 'L0_tok_W_ve', 'L0_tok_b_ve', 'L0_tok_W_lin', 'L0_tok_b_lin', 'L0_attn_basis',
        'L0_attn_shared_q_w', 'L0_attn_shared_k_w', 'L0_attn_v_coeffs', 'L0_attn_o_coeffs',
        'L0_attn_decay_logits', 'L0_attn_out_scale', 'L0_ffn_W1', 'L0_ffn_b1', 'L0_ffn_W2', 'L0_ffn_b2']


def kernel(**inputs):
    import numpy as _np
    import concourse.bacc as _bacc
    from concourse import mybir as _mybir
    from concourse.bass_utils import run_bass_kernel_spmd as _run

    nc = _bacc.Bacc("TRN2", target_bir_lowering=False, num_devices=1)
    arrays, args = {}, []
    for name in _INS:
        a = _np.ascontiguousarray(inputs[name])
        if a.ndim == 0:
            a = a.reshape(1)
        arrays[f"in_{name}_dram"] = a
        args.append(nc.dram_tensor(f"in_{name}_dram", a.shape, _mybir.dt.from_np(a.dtype), kind="ExternalInput").ap())
    args.append(nc.dram_tensor("out_dram", (B, T, D), _mybir.dt.from_np(_np.dtype("float32")),
                               kind="ExternalOutput").ap())
    build(nc, *args)
    r = _run(nc, [arrays], core_ids=[0])
    return r.results[0]["out_dram"]
```
